# Optimizing a Trainium2 kernel written in Bass

```python
import numpy as np
import jax
import jax.numpy as jnp

def _softmax(x, axis=-1):
    return jax.nn.softmax(x, axis=axis)

def _gelu(x):
    return jax.nn.gelu(x, approximate=True)

def _silu(x):
    return jax.nn.silu(x)

def _sigmoid(x):
    return jax.nn.sigmoid(x)

def _layernorm(x, axis=-1, eps=1e-05):
    m = jnp.mean(x, axis=axis, keepdims=True)
    v = jnp.var(x, axis=axis, keepdims=True)
    return (x - m) / jnp.sqrt(v + eps)

def _scatter_add(tgt, idx, src, axis=0):
    return tgt.at[idx].add(src)

def _segment_sum(src, seg, n):
    return jax.ops.segment_sum(src, seg, n)
kernel_name = 'mk_conv_preact_d1_conv_nchw128_r2_94fca1'

def setup_inputs(seed: int=0):
    np.random.seed(seed)
    _w = jnp.asarray

    def _rec_inputs():
        import jax
        import jax.numpy as jnp
        _gk = jax.random.key(seed)
        x = -0.000125 + 0.9999 * jax.random.normal(jax.random.fold_in(_gk, 1), (4, 64, 128, 128), jnp.float32)
        return x
    x = _rec_inputs()

    def _L0_conv_setup():
        import jax, jax.numpy as jnp
        import numpy as np
        import math
        B, DIM, H, W = (4, 64, 128, 128)
        HEADS, WS = (4, 8)
        C = DIM // HEADS
        HW = WS * WS

        def _forward(x, w_qkv, b_qkv, w_dw, b_dw, temperature, w_mlp, b_mlp, w_proj, b_proj):
            b, _, h, w = x.shape
            qkv = jnp.einsum('bchw,oc->bohw', x, w_qkv) + b_qkv[None, :, None, None]
            qkv = jax.lax.conv_general_dilated(qkv, w_dw, window_strides=(1, 1), padding=((1, 1), (1, 1)), feature_group_count=3 * DIM, dimension_numbers=('NCHW', 'OIHW', 'NCHW')) + b_dw[None, :, None, None]
            pad_h = (WS - h % WS) % WS
            pad_w = (WS - w % WS) % WS
            qkv = jnp.pad(qkv, ((0, 0), (0, 0), (0, pad_h), (0, pad_w)))
            Hx, Wx = (h + pad_h, w + pad_w)
            h1, w1 = (Hx // WS, Wx // WS)
            qkv = qkv.reshape(b, 3, HEADS, C, h1, WS, w1, WS)
            qkv = qkv.transpose(1, 0, 4, 6, 2, 3, 5, 7).reshape(3, b * h1 * w1, HEADS, C, HW)
            q, k, v = (qkv[0], qkv[1], qkv[2])
            attn = jnp.einsum('nhcx,nhdx->nhcd', q, k) * temperature[None]
            attn = jax.nn.softmax(attn, axis=-1)
            out = jnp.einsum('nhcd,nhdx->nhcx', attn, v)
            gate = jax.nn.gelu(jnp.einsum('nhcx,yx->nhcy', v, w_mlp) + b_mlp, approximate=False)
            out = out * gate
            out = out.reshape(b, h1, w1, HEADS, C, WS, WS)
            out = out.transpose(0, 3, 4, 1, 5, 2, 6).reshape(b, DIM, Hx, Wx)
            out = out[:, :, :h, :w]
            out = jnp.einsum('bchw,oc->bohw', out, w_proj) + b_proj[None, :, None, None]
            return out
        key = jax.random.key(seed)
        ks = jax.random.split(key, 9)
        s = 0.05
        return {'x': jax.random.normal(ks[0], (B, DIM, H, W), jnp.float32), 'w_qkv': jax.random.normal(ks[1], (3 * DIM, DIM), jnp.float32) * s, 'b_qkv': jax.random.normal(ks[2], (3 * DIM,), jnp.float32) * s, 'w_dw': jax.random.normal(ks[3], (3 * DIM, 1, 3, 3), jnp.float32) * s, 'b_dw': jax.random.normal(ks[4], (3 * DIM,), jnp.float32) * s, 'temperature': jnp.ones((HEADS, 1, 1), jnp.float32) / math.sqrt(DIM), 'w_mlp': jax.random.normal(ks[5], (HW, HW), jnp.float32) * s, 'b_mlp': jax.random.normal(ks[6], (HW,), jnp.float32) * s, 'w_proj': jax.random.normal(ks[7], (DIM, DIM), jnp.float32) * s, 'b_proj': jax.random.normal(ks[8], (DIM,), jnp.float32) * s}
    _L0_conv_all = _L0_conv_setup()
    _L0_conv_in = {k: v for k, v in _L0_conv_all.items() if k in ('w_qkv', 'b_qkv', 'w_dw', 'b_dw', 'temperature', 'w_mlp', 'b_mlp', 'w_proj', 'b_proj')}
    del _L0_conv_all
    return {'x': x, 'L0_conv_w_qkv': _L0_conv_in['w_qkv'], 'L0_conv_b_qkv': _L0_conv_in['b_qkv'], 'L0_conv_w_dw': _L0_conv_in['w_dw'], 'L0_conv_b_dw': _L0_conv_in['b_dw'], 'L0_conv_temperature': _L0_conv_in['temperature'], 'L0_conv_w_mlp': _L0_conv_in['w_mlp'], 'L0_conv_b_mlp': _L0_conv_in['b_mlp'], 'L0_conv_w_proj': _L0_conv_in['w_proj'], 'L0_conv_b_proj': _L0_conv_in['b_proj']}

def reference(x, L0_conv_w_qkv, L0_conv_b_qkv, L0_conv_w_dw, L0_conv_b_dw, L0_conv_temperature, L0_conv_w_mlp, L0_conv_b_mlp, L0_conv_w_proj, L0_conv_b_proj):
    import jax
    import jax.numpy as jnp

    def _L0_conv_ref(x, w_qkv, b_qkv, w_dw, b_dw, temperature, w_mlp, b_mlp, w_proj, b_proj):
        import jax, jax.numpy as jnp
        import numpy as np
        import math
        B, DIM, H, W = (4, 64, 128, 128)
        HEADS, WS = (4, 8)
        C = DIM // HEADS
        HW = WS * WS

        def _forward(x, w_qkv, b_qkv, w_dw, b_dw, temperature, w_mlp, b_mlp, w_proj, b_proj):
            b, _, h, w = x.shape
            qkv = jnp.einsum('bchw,oc->bohw', x, w_qkv) + b_qkv[None, :, None, None]
            qkv = jax.lax.conv_general_dilated(qkv, w_dw, window_strides=(1, 1), padding=((1, 1), (1, 1)), feature_group_count=3 * DIM, dimension_numbers=('NCHW', 'OIHW', 'NCHW')) + b_dw[None, :, None, None]
            pad_h = (WS - h % WS) % WS
            pad_w = (WS - w % WS) % WS
            qkv = jnp.pad(qkv, ((0, 0), (0, 0), (0, pad_h), (0, pad_w)))
            Hx, Wx = (h + pad_h, w + pad_w)
            h1, w1 = (Hx // WS, Wx // WS)
            qkv = qkv.reshape(b, 3, HEADS, C, h1, WS, w1, WS)
            qkv = qkv.transpose(1, 0, 4, 6, 2, 3, 5, 7).reshape(3, b * h1 * w1, HEADS, C, HW)
            q, k, v = (qkv[0], qkv[1], qkv[2])
            attn = jnp.einsum('nhcx,nhdx->nhcd', q, k) * temperature[None]
            attn = jax.nn.softmax(attn, axis=-1)
            out = jnp.einsum('nhcd,nhdx->nhcx', attn, v)
            gate = jax.nn.gelu(jnp.einsum('nhcx,yx->nhcy', v, w_mlp) + b_mlp, approximate=False)
            out = out * gate
            out = out.reshape(b, h1, w1, HEADS, C, WS, WS)
            out = out.transpose(0, 3, 4, 1, 5, 2, 6).reshape(b, DIM, Hx, Wx)
            out = out[:, :, :h, :w]
            out = jnp.einsum('bchw,oc->bohw', out, w_proj) + b_proj[None, :, None, None]
            return out
        return _forward(x, w_qkv, b_qkv, w_dw, b_dw, temperature, w_mlp, b_mlp, w_proj, b_proj)

    def _gn(v, G=32, eps=1e-05):
        B_, C_, H_, W_ = v.shape
        g = v.reshape(B_, G, C_ // G, H_, W_)
        m = jnp.mean(g, axis=(2, 3, 4), keepdims=True)
        s = jnp.var(g, axis=(2, 3, 4), keepdims=True)
        return ((g - m) / jnp.sqrt(s + eps)).reshape(v.shape)

    def _ln_c(v, eps=1e-06):
        m = jnp.mean(v, axis=1, keepdims=True)
        s = jnp.var(v, axis=1, keepdims=True)
        return (v - m) / jnp.sqrt(s + eps)

    def _ln_t(v, eps=1e-05):
        m = jnp.mean(v, axis=-1, keepdims=True)
        s = jnp.var(v, axis=-1, keepdims=True)
        return (v - m) / jnp.sqrt(s + eps)

    def _to_tokens(v):
        B_, C_, H_, W_ = v.shape
        return v.reshape(B_, C_, H_ * W_).transpose(0, 2, 1)

    def _from_tokens(t, like):
        B_, C_, H_, W_ = like.shape
        return t.transpose(0, 2, 1).reshape(B_, C_, H_, W_)
    x = x + _L0_conv_ref(_gn(x), L0_conv_w_qkv, L0_conv_b_qkv, L0_conv_w_dw, L0_conv_b_dw, L0_conv_temperature, L0_conv_w_mlp, L0_conv_b_mlp, L0_conv_w_proj, L0_conv_b_proj)
    return x

_drawn_inputs = setup_inputs


def setup_inputs(seed=0):
    import zlib

    import numpy as np

    out = dict(_drawn_inputs(seed))
    spreads = {'L0_conv_temperature': (0.125, 0.6)}
    factors = {'L0_conv_w_qkv': 8.0,
     'L0_conv_b_qkv': 8.0,
     'L0_conv_w_dw': 8.0,
     'L0_conv_b_dw': 8.0,
     'L0_conv_w_mlp': 8.0,
     'L0_conv_b_mlp': 8.0,
     'L0_conv_w_proj': 8.0,
     'L0_conv_b_proj': 64.0}
    for name, (base, spread) in spreads.items():
        noise = np.random.default_rng([zlib.crc32(name.encode()), seed]).standard_normal(out[name].shape)
        drawn = base * np.exp(spread * noise) if base else spread * noise
        out[name] = jnp.asarray(drawn.astype(out[name].dtype))
    for name, factor in factors.items():
        out[name] = (out[name] * factor).astype(out[name].dtype)
    return out
```

```python
from contextlib import ExitStack

import numpy as np

import concourse.bass as bass
from concourse import mybir

ALU = mybir.AluOpType
ACT = mybir.ActivationFunctionType
F32 = mybir.dt.float32
F16 = mybir.dt.float16
AX_X = mybir.AxisListType.X
ABSMAX = bass.bass_isa.ReduceOp.absmax

B, C, H, W = 4, 64, 128, 128
HEADS, WS = 4, 8
HW = WS * WS
QKV = 3 * C
P = 2 * C
PAIRS = B // 2
TAPS = 9
EPS = 1e-5

GROUPS = 4
GW = WS
STRIP = GROUPS * GW
BAND = 2 * WS
STRIPS = W // STRIP
BANDS = H // BAND
STEPS = PAIRS * BANDS * STRIPS
PAIR_STEPS = BANDS * STRIPS
PW = W + 2
PIX = PW * (H + 2)
HR, HC = BAND + 2, STRIP + 2
NP = BAND * GW
PASSES = 14
NPIX = GROUPS * P
WINDOWS = 2 * GROUPS
CHUNKS = BANDS
STAT_ROWS = 512 // W
STATS = H // STAT_ROWS
WSCALE = 1024.0
XSCALE = 64.0
BIAS_ROWS = 32
NEG = -1.0e38
TINY = 1.0e-30


def wait(engine, semaphore, value):
    if isinstance(value, int) and value <= 0:
        return
    engine.wait_ge(semaphore, value)


def build(nc, x, w_qkv_t, w_dw_rows, b_qkv_rows, b_dw_rows, out_scale_rows, bias_a, bias_d,
          w_mlp_bd, b_mlp_rows, w_proj_bd, b_proj_col, ident_c, group_c, mask_c, rows_in, cols_in,
          split_c, out):
    with ExitStack() as ctx:
        def sb(name, shape, dt=F32):
            return ctx.enter_context(nc.sbuf_tensor(name, shape, dt))

        def psum(name):
            return ctx.enter_context(nc.psum_tensor(name, [P, 512], F32))

        def sem(name):
            return ctx.enter_context(nc.semaphore(name))

        X = sb("X", [P, PAIRS * PIX])
        Xv = X[:].rearrange("p (j r c) -> p j r c", j=PAIRS, c=PW)
        Xr = X[:].rearrange("p (r c) -> p r c", c=PW)
        T = sb("T", [P, HR, HC])
        high_n = sb("high_n", [P, HR, HC], F16)
        low_n = sb("low_n", [P, HR, HC], F16)
        full, part = [P, 2, 2, GROUPS, HR * GW], [P, 2, 2, GROUPS, NP]
        high01 = sb("high01", full, F16)
        high2low0 = sb("high2low0", full, F16)
        high2low1 = sb("high2low1", full, F16)
        low2rows = sb("low2rows", part, F16)
        low2inside = sb("low2inside", part, F16)
        conv_w = sb("conv_w", [P, PASSES, QKV], F16)
        unscale = sb("unscale", [P, QKV])
        qkv = sb("qkv", [P, 2, GROUPS, 3, 2, C])
        scores = sb("scores", [P, WINDOWS, C])
        probs = scores
        probs_bd = sb("probs_bd", [P, GROUPS, 2, P])
        v_t = sb("v_t", [P, NPIX])
        gate = sb("gate", [P, NPIX])
        mixed = v_t[:].rearrange("p (r c) -> p r c", c=STRIP)
        neg_max = sb("neg_max", [P, WINDOWS])
        total = sb("total", [P, WINDOWS])
        inv_total = sb("inv_total", [P, WINDOWS])
        staged = sb("staged", [P, 2, BAND, W])
        ident = sb("ident", [P, P])
        group_mean = sb("group_mean", [P, P])
        mlp = sb("mlp", [P, P])
        proj = sb("proj", [P, P])
        b_mlp = sb("b_mlp", [P, HW])
        b_proj = sb("b_proj", [P, 1])
        head_mask = sb("head_mask", [P, C])
        in_rows = sb("in_rows", [P, H], F16)
        in_cols = sb("in_cols", [P, W], F16)
        split = sb("split", [P, 2])
        stats = sb("stats", [P, STATS, 6])
        mean_var = sb("mean_var", [P, 2])
        small = sb("small", [P, 8])
        norm = sb("norm", [P, 2])
        scratch = staged[:].rearrange("p a b c -> p (a b c)")
        w_dw_b = scratch[:, 0:TAPS * QKV]
        w_full = scratch[:, TAPS * QKV:2 * TAPS * QKV]
        w_t = scratch[:, 2 * TAPS * QKV:2 * TAPS * QKV + QKV]
        w_max = scratch[:, 2 * TAPS * QKV + QKV:2 * TAPS * QKV + 2 * QKV]
        high_w = w_dw_b[:, 0:TAPS * QKV // 2].bitcast(F16)
        low_w = w_dw_b[:, TAPS * QKV // 2:TAPS * QKV].bitcast(F16)
        dw_max, chan = gate[:, 0:QKV], gate[:, QKV:2 * QKV]
        b_dw_b, scale_b = v_t[:, 0:QKV], v_t[:, QKV:2 * QKV]
        bias = slice(C, C + BIAS_ROWS)
        scores_f = scores[:].rearrange("p w c -> p (w c)")
        bias_a_s, bias_d_s = scores_f[bias, 0:QKV], scores_f[bias, QKV:2 * QKV]
        probs_bd_f = probs_bd[:].rearrange("p g u c -> p (g u c)")
        bias_lo, bias_hi_f = probs_bd_f[bias, 0:QKV], probs_bd_f[bias, QKV:2 * QKV]
        bias_hi = probs_bd_f[bias, 4 * QKV:4 * QKV + QKV // 2].bitcast(F16)
        inv_chan, b_qkv_b = probs_bd_f[:, 2 * QKV:3 * QKV], probs_bd_f[:, 3 * QKV:4 * QKV]

        conv_ps = [psum("conv_ps0"), psum("conv_ps1")]
        scores_ps = psum("scores_ps")
        gate_ps = psum("gate_ps")
        v_t_ps = psum("v_t_ps")
        probs_t_ps = psum("probs_t_ps")
        mix_ps = psum("mix_ps")
        proj_ps = psum("proj_ps")

        x_in = [sem(f"x_in{n}") for n in range(CHUNKS)]
        x_in_next = sem("x_in_next")
        weights_in = sem("weights_in")
        consts_in = sem("consts_in")
        w_max_ready = sem("w_max_ready")
        borders_clear = sem("borders_clear")
        bd_clear = sem("bd_clear")
        setup = sem("setup")
        group_mean_done = sem("group_mean_done")
        centred = sem("centred")
        group_var_done = sem("group_var_done")
        var_ready = sem("var_ready")
        dev_ready = sem("dev_ready")
        norm_chain = sem("norm_chain")
        norm_ready = sem("norm_ready")
        high_ready = sem("high_ready")
        low_ready = sem("low_ready")
        operands_ready = sem("operands_ready")
        inside_ready = sem("inside_ready")
        conv_done = sem("conv_done")
        qkv_ready = sem("qkv_ready")
        gate_done = sem("gate_done")
        v_t_done = sem("v_t_done")
        scores_done = sem("scores_done")
        masked = sem("masked")
        max_ready = sem("max_ready")
        shifted = sem("shifted")
        exp_ready = sem("exp_ready")
        total_ready = sem("total_ready")
        inv_ready = sem("inv_ready")
        probs_ready = sem("probs_ready")
        probs_t_done = sem("probs_t_done")
        probs_bd_ready = sem("probs_bd_ready")
        v_t_ready = sem("v_t_ready")
        gate_biased = sem("gate_biased")
        gate_ready = sem("gate_ready")
        mix_done = sem("mix_done")
        mixed_ready = sem("mixed_ready")
        proj_done = sem("proj_done")
        out_ready = sem("out_ready")
        staged_free = sem("staged_free")
        stored = staged_free

        def patch(s, r0, c0, rows, cols):
            row = ((s >> 2) & (PAIRS * BANDS - 1)) * BAND + ((s >> 5) & (PAIRS - 1)) * 2
            return Xr[:, bass.ds(row + r0, rows), bass.ds((s & 3) * STRIP + c0, cols)]

        block = ctx.enter_context(nc.Block())

        @block.sync
        def _(sp):
            halves = x.rearrange("(j b) c h w -> j (b c) h w", j=PAIRS)
            rows = H // CHUNKS
            for n in range(CHUNKS):
                sp.dma_start(Xv[:, 0, 1 + n * rows:1 + (n + 1) * rows, 1:1 + W],
                             halves[0, :, n * rows:(n + 1) * rows, :]).then_inc(x_in[n], 16)
            for n in range(CHUNKS):
                sp.dma_start(Xv[:, 1, 1 + n * rows:1 + (n + 1) * rows, 1:1 + W],
                             halves[1, :, n * rows:(n + 1) * rows, :]).then_inc(x_in_next, 16)
            bands = out.rearrange("(j b) c h w -> j (b c) h w", j=PAIRS)
            for j in range(PAIRS):
                with sp.Fori(0, BANDS // 2) as i:
                    for k in range(2):
                        sp.wait_ge(out_ready, (i * 2 + (j * BANDS + k + 1)) * STRIPS)
                        sp.wait_ge(stored, (i * 2 + (j * BANDS + k + 2)) * 16)
                        sp.dma_start(bands[j, :, bass.ds((i * 2 + k) * BAND, BAND), :],
                                     staged[:, k]).then_inc(stored, 16)
            sp.wait_ge(stored, 16 * (2 + PAIRS * BANDS))

        @block.gpsimd
        def _(pool):
            nc.gpsimd.memset(Xv[:, :, 0:H + 2:H + 1, :], 0.0)
            nc.gpsimd.memset(Xv[:, :, 1:H + 1, 0:PW:PW - 1], 0.0).then_inc(borders_clear, 1)
            nc.gpsimd.memset(small[:, 6:7], 0.0).then_inc(staged_free, 32)
            pool.wait_ge(weights_in, 16 * 8)
            nc.gpsimd.partition_all_reduce(w_max, w_t, P, ABSMAX).then_inc(w_max_ready, 1)
            pool.wait_ge(setup, 24)
            nc.gpsimd.memset(probs_bd[:], 0.0).then_inc(bd_clear, 1)
            pool.wait_ge(bd_clear, 1)
            pool.wait_ge(consts_in, 16 * 10)

            def inside(s, k):
                wait(pool, conv_done, (s - 1) * GROUPS)
                r = in_rows[bias, bass.ds(((s >> 2) & (BANDS - 1)) * BAND, BAND)]
                c = in_cols[bias, bass.ds((s & (STRIPS - 1)) * STRIP, STRIP)].rearrange("p (g c) -> p g c", c=GW)
                over = [BIAS_ROWS, GROUPS, BAND, GW]
                for t in range(2):
                    last = nc.gpsimd.tensor_tensor(
                        low2inside[bias, k, t].rearrange("p g (r c) -> p g r c", c=GW),
                        r.unsqueeze(1).unsqueeze(3).to_broadcast(over), c.unsqueeze(2).to_broadcast(over), ALU.mult)
                last.then_inc(inside_ready, 1)

            inside(0, 0)
            inside(1, 1)
            with pool.Fori(1, STEPS // 2) as i:
                for k in range(2):
                    inside(i * 2 + k, k)

        @block.scalar
        def _(act):
            act.dma_start(w_t[0:C], w_qkv_t).then_inc(weights_in, 16)
            act.dma_start(w_t[C:P], w_qkv_t).then_inc(weights_in, 16)
            act.dma_start(w_dw_b, w_dw_rows).then_inc(weights_in, 16)
            act.dma_start(b_qkv_b, b_qkv_rows).then_inc(weights_in, 16)
            act.dma_start(b_dw_b, b_dw_rows).then_inc(weights_in, 16)
            act.dma_start(scale_b, out_scale_rows).then_inc(weights_in, 16)
            act.dma_start(bias_a_s, bias_a).then_inc(weights_in, 16)
            act.dma_start(bias_d_s, bias_d).then_inc(weights_in, 16)
            for to, of in ((group_mean[:], group_c), (ident[:], ident_c), (mlp[:], w_mlp_bd),
                           (proj[:], w_proj_bd), (b_mlp[:], b_mlp_rows), (b_proj[:], b_proj_col),
                           (head_mask[:], mask_c), (in_rows[bias], rows_in),
                           (in_cols[bias], cols_in), (split[bias], split_c)):
                act.dma_start(to, of).then_inc(consts_in, 16)

            def deviation(n):
                act.wait_ge(var_ready, n)
                nc.scalar.activation(small[:, 3:4], small[:, 2:3], ACT.Sqrt).then_inc(dev_ready, 1)

            def high(s):
                act.wait_ge(norm_ready, s + 1)
                wait(act, operands_ready, s)
                nc.scalar.activation(high_n[:], T[:], ACT.Copy).then_inc(high_ready, 1)

            def step(s, k, prepare=True):
                act.wait_ge(shifted, s)
                nc.scalar.activation(probs[:], scores[:], ACT.Exp).then_inc(exp_ready, 1)
                if prepare:
                    high(s + 1)
                act.wait_ge(gate_biased, s)
                nc.scalar.activation(gate[:], gate[:], ACT.Gelu).then_inc(gate_ready, 1)
                act.wait_ge(probs_t_done, s)
                wait(act, mix_done, s - 1)
                for t in range(2):
                    h = slice(t * C, t * C + C)
                    last = nc.scalar.activation(
                        probs_bd[h, :, :, h], probs_t_ps[h, :].rearrange("p (g u c) -> p g u c", g=GROUPS, u=2),
                        ACT.Copy)
                last.then_inc(probs_bd_ready, 1)

            deviation(1)
            high(0)
            high(1)
            act.wait_ge(bd_clear, 1)
            step(1, 1)
            with act.Fori(1, (PAIR_STEPS - 2) // 2) as i:
                for k in range(2):
                    step(i * 2 + k, k)
            step(PAIR_STEPS - 2, 0)
            deviation(2)
            step(PAIR_STEPS - 1, 1)
            with act.Fori(PAIR_STEPS // 2, STEPS // 2 - 1) as i:
                for k in range(2):
                    step(i * 2 + k, k)
            step(STEPS - 2, 0)
            step(STEPS - 1, 1, prepare=False)
            step(STEPS, 0, prepare=False)

        @block.vector
        def _(dve):
            count = [0]

            def link(ins):
                count[0] += 1
                ins.then_inc(setup, 1)
                dve.wait_ge(setup, count[0])

            def statistics(pair, n):
                rows = Xr[:, bass.ds(n * STAT_ROWS + (pair * (H + 2) + 1), STAT_ROWS), 1:1 + W]
                return nc.vector.bn_stats(stats[:, bass.ds(n, 1), :], rows)

            def normaliser(pair):
                c0 = pair * 7
                dve.wait_ge(borders_clear, 1)
                link(nc.vector.bn_aggr(mean_var[:], stats[:].rearrange("p n k -> p (n k)")))
                dve.wait_ge(group_mean_done, pair + 1)
                if pair:
                    dve.wait_ge(norm_ready, PAIR_STEPS)
                nc.vector.tensor_copy(norm[:, 0:1], proj_ps[:, 0:1]).then_inc(norm_chain, 1)
                dve.wait_ge(norm_chain, c0 + 1)
                nc.vector.tensor_tensor(small[:, 0:1], mean_var[:, 0:1], norm[:, 0:1],
                                        ALU.subtract).then_inc(norm_chain, 1)
                dve.wait_ge(norm_chain, c0 + 2)
                nc.vector.scalar_tensor_tensor(small[:, 1:2], small[:, 0:1], small[:, 0:1], mean_var[:, 1:2],
                                               op0=ALU.mult, op1=ALU.add).then_inc(centred, 1)
                dve.wait_ge(group_var_done, pair + 1)
                nc.vector.tensor_scalar(small[:, 2:3], proj_ps[:, 1:2], EPS, None, ALU.add).then_inc(var_ready, 1)
                dve.wait_ge(dev_ready, pair + 1)
                nc.vector.reciprocal(small[:, 4:5], small[:, 3:4]).then_inc(norm_chain, 1)
                dve.wait_ge(norm_chain, c0 + 3)
                nc.vector.scalar_tensor_tensor(small[:, 5:6], small[:, 4:5], small[:, 4:5], small[:, 2:3],
                                               op0=ALU.mult, op1=ALU.mult).then_inc(norm_chain, 1)
                dve.wait_ge(norm_chain, c0 + 4)
                nc.vector.tensor_scalar(small[:, 5:6], small[:, 5:6], -0.5 * XSCALE, 1.5 * XSCALE,
                                        ALU.mult, ALU.add).then_inc(norm_chain, 1)
                dve.wait_ge(norm_chain, c0 + 5)
                nc.vector.tensor_tensor(norm[:, 1:2], small[:, 4:5], small[:, 5:6], ALU.mult).then_inc(norm_chain, 1)
                for edge in (Xv[:, pair, 0:H + 2:H + 1, :], Xv[:, pair, 1:H + 1, 0:PW:PW - 1]):
                    last = nc.vector.tensor_scalar(edge, edge, norm[:, 0:1], None, ALU.add)
                last.then_inc(norm_chain, 1)
                dve.wait_ge(norm_chain, c0 + 7)

            def normalise(s):
                wait(dve, high_ready, s)
                wait(dve, operands_ready, s)
                nc.vector.tensor_scalar(T[:], patch(s, 0, 0, HR, HC), norm[:, 0:1], norm[:, 1:2],
                                        ALU.subtract, ALU.mult).then_inc(norm_ready, 1)

            def operands(s, k):
                dve.wait_ge(high_ready, s + 1)
                nc.vector.tensor_tensor(low_n[:], T[:], high_n[:], ALU.subtract).then_inc(low_ready, 1)
                dve.wait_ge(low_ready, s + 1)
                wait(dve, conv_done, (s - 1) * GROUPS)
                upper, lower = slice(0, C), slice(C, P)
                for t in range(2):
                    image = slice(t * C, t * C + C)
                    for to, half, of, col, row in (
                            (high01, upper, high_n, 0, 0), (high01, lower, high_n, 1, 0),
                            (high2low0, upper, high_n, 2, 0), (high2low0, lower, low_n, 0, 0),
                            (high2low1, upper, high_n, 2, 0), (high2low1, lower, low_n, 1, 0),
                            (low2rows, upper, low_n, 2, 0), (low2rows, lower, low_n, 2, 1),
                            (low2inside, upper, low_n, 2, 2)):
                        to = to[half, k, t].rearrange("p g (r c) -> p g r c", c=GW)
                        of = of[image, row:row + to.shape[2], col:col + STRIP]
                        last = nc.vector.tensor_copy(to, of.rearrange("p r (g c) -> p g r c", c=GW))
                last.then_inc(operands_ready, 1)

            def evacuate(s, k, g):
                dve.wait_ge(conv_done, s * GROUPS + (g + 1))
                nc.vector.tensor_tensor(
                    qkv[:, k, g].rearrange("p k t c -> p t k c"),
                    conv_ps[g % 2][:, 0:2 * QKV].rearrange("p (t k c) -> p t k c", t=2, k=3),
                    unscale[:].rearrange("p (k c) -> p k c", k=3).unsqueeze(1).to_broadcast([P, 2, 3, C]),
                    ALU.mult).then_inc(qkv_ready, 1)

            def mix(s):
                dve.wait_ge(mix_done, s - 1)
                dve.wait_ge(gate_ready, s - 1)
                wait(dve, proj_done, s - 2)
                nc.vector.tensor_tensor(
                    mixed.rearrange("p r (g c) -> p g r c", g=GROUPS),
                    mix_ps[:].rearrange("p (g r c) -> p g r c", g=GROUPS, c=GW),
                    gate[:].rearrange("p (g r c) -> p g r c", g=GROUPS, c=GW), ALU.mult).then_inc(mixed_ready, 1)

            def scores_up(s):
                dve.wait_ge(scores_done, s)
                wait(dve, probs_t_done, s - 1)
                nc.vector.tensor_tensor(
                    scores[:], scores_ps[:].rearrange("p (w c) -> p w c", c=C),
                    head_mask[:].unsqueeze(1).to_broadcast([P, WINDOWS, C]), ALU.add).then_inc(masked, 1)
                dve.wait_ge(masked, s)
                nc.vector.tensor_reduce(neg_max[:], scores[:], AX_X, ALU.max, negate=True).then_inc(max_ready, 1)
                dve.wait_ge(max_ready, s)
                nc.vector.tensor_tensor(scores[:], scores[:],
                                        neg_max[:].unsqueeze(2).to_broadcast([P, WINDOWS, C]),
                                        ALU.add).then_inc(shifted, 1)

            def gate_up(s):
                dve.wait_ge(gate_done, s)
                wait(dve, mixed_ready, s - 1)
                nc.vector.tensor_tensor(
                    gate[:].rearrange("p (w y) -> p w y", y=HW), gate_ps[:].rearrange("p (w y) -> p w y", y=HW),
                    b_mlp[:].unsqueeze(1).to_broadcast([P, WINDOWS, HW]), ALU.add).then_inc(gate_biased, 1)

            def v_up(s):
                dve.wait_ge(v_t_done, s)
                wait(dve, mix_done, s - 1)
                wait(dve, proj_done, s - 1)
                nc.vector.tensor_copy(v_t[:], v_t_ps[:]).then_inc(v_t_ready, 1)

            def divide(s):
                dve.wait_ge(exp_ready, s)
                nc.vector.tensor_reduce(total[:], probs[:], AX_X, ALU.add).then_inc(total_ready, 1)
                dve.wait_ge(total_ready, s)
                nc.vector.reciprocal(inv_total[:], total[:]).then_inc(inv_ready, 1)
                dve.wait_ge(inv_ready, s)
                nc.vector.tensor_tensor(probs[:], probs[:],
                                        inv_total[:].unsqueeze(2).to_broadcast([P, WINDOWS, C]),
                                        ALU.mult).then_inc(probs_ready, 1)

            def residual(s):
                r = s - 2
                dve.wait_ge(proj_done, s - 1)
                dve.wait_ge(staged_free, ((r >> 2) + 1) * 16)
                to = staged[:].rearrange("p a r w -> p (a r) w")
                to = to[:, bass.ds(((r >> 2) & 1) * BAND, BAND), bass.ds((r & 3) * STRIP, STRIP)]
                nc.vector.scalar_tensor_tensor(to, proj_ps[:].rearrange("p (r c) -> p r c", c=STRIP), b_proj[:, 0:1],
                                               patch(r, 1, 1, BAND, STRIP), op0=ALU.add,
                                               op1=ALU.add).then_inc(out_ready, 1)

            def step(s, k, conv=True, prepare=True, attend=True, finish=True, more=()):
                if finish:
                    mix(s)
                if conv:
                    evacuate(s, k, 0)
                if prepare:
                    normalise(s + 1)
                if attend:
                    scores_up(s)
                    gate_up(s)
                if conv:
                    evacuate(s, k, 1)
                if finish:
                    residual(s)
                if attend:
                    v_up(s)
                    divide(s)
                if conv:
                    evacuate(s, k, 2)
                if prepare:
                    operands(s + 1, 1 - k)
                for pair, n in more:
                    statistics(pair, n)
                if conv:
                    evacuate(s, k, 3)

            for n in range(CHUNKS):
                dve.wait_ge(x_in[n], 16)
                for m in range(STATS // CHUNKS):
                    last = statistics(0, n * (STATS // CHUNKS) + m)
            link(last)
            dve.wait_ge(consts_in, 16 * 10)
            normaliser(0)
            normalise(0)
            dve.wait_ge(weights_in, 16 * 8)
            dve.wait_ge(w_max_ready, 1)
            link(nc.vector.tensor_reduce(dw_max, w_dw_b.rearrange("p (t o) -> p o t", t=TAPS), AX_X, ALU.max,
                                         apply_absolute_value=True))
            for b in (b_qkv_b, b_dw_b):
                last = nc.vector.scalar_tensor_tensor(b, b, -1.0, b, op0=ALU.mult, op1=ALU.max)
            link(last)
            link(nc.vector.tensor_tensor(chan, w_max, b_qkv_b, ALU.max))
            link(nc.vector.tensor_tensor(chan, chan, dw_max, ALU.mult))
            link(nc.vector.tensor_tensor(chan, chan, b_dw_b, ALU.max))
            link(nc.vector.tensor_scalar(chan, chan, TINY, None, ALU.max))
            link(nc.vector.reciprocal(inv_chan, chan))
            link(nc.vector.tensor_tensor(unscale[:], chan, scale_b, ALU.mult))
            link(nc.vector.tensor_scalar(unscale[:], unscale[:], 1.0 / (WSCALE * XSCALE), None, ALU.mult))
            link(nc.vector.tensor_scalar(inv_chan, inv_chan, WSCALE, None, ALU.mult))
            over = [P, TAPS, QKV]
            wf = w_full.rearrange("p (t o) -> p t o", t=TAPS)
            link(nc.vector.tensor_tensor(wf, w_dw_b.rearrange("p (t o) -> p t o", t=TAPS),
                                         w_t.unsqueeze(1).to_broadcast(over), ALU.mult))
            link(nc.vector.tensor_tensor(wf, wf, inv_chan.unsqueeze(1).to_broadcast(over), ALU.mult))
            hw, lw = (w.rearrange("p (y x o) -> p y x o", y=3, x=3) for w in (high_w, low_w))
            link(nc.vector.tensor_copy(high_w.rearrange("p (t o) -> p t o", t=TAPS), wf))
            link(nc.vector.tensor_tensor(low_w.rearrange("p (t o) -> p t o", t=TAPS), wf,
                                         high_w.rearrange("p (t o) -> p t o", t=TAPS), ALU.subtract))
            up, down = slice(0, C), slice(C, P)
            for first, half, of, col in ((0, up, hw, 0), (0, down, hw, 1), (3, up, lw, 0), (3, down, lw, 1),
                                         (6, up, hw, 2), (6, down, hw, 0), (9, up, lw, 2), (9, down, hw, 1)):
                nc.vector.tensor_copy(conv_w[half, first:first + 3, :], of[half, :, col, :])
            nc.vector.tensor_copy(conv_w[up, 12, :], hw[up, 0, 2, :])
            nc.vector.tensor_copy(conv_w[down, 12, :], hw[down, 1, 2, :])
            link(nc.vector.tensor_copy(conv_w[up, 13, :], hw[up, 2, 2, :]))
            link(nc.vector.tensor_tensor(bias_a_s, bias_a_s, bias_d_s, ALU.mult))
            link(nc.vector.tensor_tensor(bias_a_s, bias_a_s, inv_chan[bias], ALU.mult))
            link(nc.vector.tensor_copy(bias_hi, bias_a_s))
            link(nc.vector.tensor_tensor(bias_lo, bias_a_s, bias_hi, ALU.subtract))
            link(nc.vector.tensor_scalar(bias_hi_f, bias_hi, split[bias, 0:1], None, ALU.mult))
            link(nc.vector.scalar_tensor_tensor(conv_w[bias, 13, :], bias_lo, split[bias, 1:2], bias_hi_f,
                                                op0=ALU.mult, op1=ALU.add))
            link(nc.vector.memset(total[:], 0.0))
            assert count[0] == 24, count[0]
            operands(0, 0)
            step(0, 0, attend=False, finish=False)
            step(1, 1, finish=False)
            stat_from = PAIR_STEPS - 2 - STATS // 2
            with dve.Fori(1, stat_from // 2) as i:
                for k in range(2):
                    step(i * 2 + k, k)
            dve.wait_ge(x_in_next, 16 * CHUNKS)
            with dve.Fori(stat_from // 2, (PAIR_STEPS - 2) // 2) as i:
                for k in range(2):
                    step(i * 2 + k, k, more=[(1, i * 4 + (2 * k + m - 2 * stat_from)) for m in range(2)])
            step(PAIR_STEPS - 2, 0)
            normaliser(1)
            step(PAIR_STEPS - 1, 1)
            with dve.Fori(PAIR_STEPS // 2, STEPS // 2 - 1) as i:
                for k in range(2):
                    step(i * 2 + k, k)
            step(STEPS - 2, 0)
            step(STEPS - 1, 1, prepare=False)
            step(STEPS, 0, conv=False, prepare=False)
            step(STEPS + 1, 1, conv=False, prepare=False, attend=False)

        @block.tensor
        def _(pe):
            def group_stats(n):
                pe.wait_ge(setup, 2 if n == 1 else 25)
                wait(pe, out_ready, 0 if n == 1 else PAIR_STEPS - 3)
                nc.tensor.matmul(proj_ps[:, 0:1], group_mean[:], mean_var[:, 0:1], start=True,
                                 stop=True).then_inc(group_mean_done, 1)
                pe.wait_ge(centred, n)
                nc.tensor.matmul(proj_ps[:, 1:2], group_mean[:], small[:, 1:2], start=True,
                                 stop=True).then_inc(group_var_done, 1)

            def conv(s, k, g):
                if g == 0:
                    pe.wait_ge(operands_ready, s + 1)
                    pe.wait_ge(inside_ready, s + 1)
                wait(pe, qkv_ready, s * GROUPS + (g - 1))
                for t in range(2):
                    def rows(tensor, y=0, p=P):
                        return tensor[0:p, k, t, g, y * GW:y * GW + NP]
                    passes = [rows(high01, y) for y in range(3)] * 2
                    passes += [rows(high2low0, y) for y in range(3)] + [rows(high2low1, y) for y in range(3)]
                    passes += [rows(low2rows), rows(low2inside, p=C + BIAS_ROWS)]
                    for n, pixels in enumerate(passes):
                        last = nc.tensor.matmul(conv_ps[g % 2][:, t * QKV:(t + 1) * QKV], pixels,
                                                conv_w[0:pixels.shape[0], n, :],
                                                start=(n == 0), stop=(n == len(passes) - 1))
                last.then_inc(conv_done, 1)

            def attend(s, k):
                pe.wait_ge(qkv_ready, s * GROUPS)
                wait(pe, gate_biased, s - 1)
                wait(pe, v_t_ready, s - 1)
                wait(pe, masked, s - 1)
                for g in range(GROUPS):
                    v = qkv[:, k, g, 2].rearrange("p t c -> p (t c)")
                    last = nc.tensor.matmul(gate_ps[:, g * P:(g + 1) * P], v, mlp[:], start=True, stop=True)
                last.then_inc(gate_done, 1)
                for g in range(GROUPS):
                    for t in range(2):
                        for u in range(2):
                            h = slice(u * C, u * C + C)
                            last = nc.tensor.matmul(
                                scores_ps[h, (2 * g + t) * C:(2 * g + t + 1) * C], qkv[h, k, g, 0, t, :],
                                qkv[h, k, g, 1, t, :], start=True, stop=True)
                last.then_inc(scores_done, 1)
                for g in range(GROUPS):
                    v = qkv[:, k, g, 2].rearrange("p t c -> p (t c)")
                    last = nc.tensor.transpose(v_t_ps[:, g * P:(g + 1) * P], v, ident[:])
                last.then_inc(v_t_done, 1)

            def turn_probs(s):
                pe.wait_ge(probs_ready, s)
                wait(pe, probs_bd_ready, s - 1)
                for g in range(GROUPS):
                    last = nc.tensor.transpose(probs_t_ps[:, g * P:(g + 1) * P],
                                               probs[:, 2 * g:2 * g + 2, :].rearrange("p t c -> p (t c)"), ident[:])
                last.then_inc(probs_t_done, 1)

            def apply_probs(s):
                pe.wait_ge(probs_bd_ready, s)
                pe.wait_ge(v_t_ready, s)
                wait(pe, mixed_ready, s - 1)
                for g in range(GROUPS):
                    for u in range(2):
                        at = slice(g * P + u * HW, g * P + (u + 1) * HW)
                        last = nc.tensor.matmul(mix_ps[:, at], probs_bd[:, g, u, :], v_t[:, at], start=True, stop=True)
                last.then_inc(mix_done, 1)

            def project(s):
                pe.wait_ge(mixed_ready, s - 1)
                wait(pe, out_ready, s - 2)
                nc.tensor.matmul(proj_ps[:], proj[:], mixed.rearrange("p r c -> p (r c)"), start=True,
                                 stop=True).then_inc(proj_done, 1)

            def step(s, k, convolve=True, attention=True, finish=True):
                if convolve:
                    conv(s, k, 0)
                if attention:
                    attend(s, 1 - k)
                if convolve:
                    conv(s, k, 1)
                if finish:
                    project(s)
                if convolve:
                    conv(s, k, 2)
                if attention:
                    turn_probs(s)
                if convolve:
                    conv(s, k, 3)
                if attention:
                    apply_probs(s)

            pe.wait_ge(consts_in, 16 * 10)
            group_stats(1)
            step(0, 0, attention=False, finish=False)
            step(1, 1, finish=False)
            with pe.Fori(1, (PAIR_STEPS - 2) // 2) as i:
                for k in range(2):
                    step(i * 2 + k, k)
            step(PAIR_STEPS - 2, 0)
            group_stats(2)
            step(PAIR_STEPS - 1, 1)
            with pe.Fori(PAIR_STEPS // 2, STEPS // 2) as i:
                for k in range(2):
                    step(i * 2 + k, k)
            step(STEPS, 0, convolve=False)
            step(STEPS + 1, 1, convolve=False, attention=False)


_ORDER = ("x", "w_qkv_t", "w_dw_rows", "b_qkv_rows", "b_dw_rows", "out_scale_rows", "bias_a", "bias_d",
          "w_mlp_bd", "b_mlp_rows", "w_proj_bd", "b_proj_col", "ident", "group", "mask", "rows_in",
          "cols_in", "split")


def _constants():
    f = np.float32
    chan = np.arange(P)
    head = np.arange(C) // (C // HEADS)
    tap = np.arange(16)
    dy, dx = tap // 3 - 1, tap % 3 - 1
    dy[TAPS:], dx[TAPS:] = 0, 0
    at = np.arange(H)
    rows = ((at + dy[:, None] >= 0) & (at + dy[:, None] < H)) * XSCALE
    cols = ((at + dx[:, None] >= 0) & (at + dx[:, None] < W)) * 1.0
    rows[TAPS + 1:] = 0
    return {
        "ident": np.eye(P, dtype=f),
        "group": (0.5 * (chan[:, None] // 2 == chan[None, :] // 2)).astype(f),
        "mask": np.tile(np.where(head[:, None] == head[None, :], 0.0, NEG), (2, 1)).astype(f),
        "rows_in": np.tile(rows, (2, 1)).astype(np.float16),
        "cols_in": np.tile(cols, (2, 1)).astype(np.float16),
        "split": np.repeat(np.eye(2, dtype=f), 16, axis=0),
    }


def kernel(x, L0_conv_w_qkv, L0_conv_b_qkv, L0_conv_w_dw, L0_conv_b_dw, L0_conv_temperature, L0_conv_w_mlp,
           L0_conv_b_mlp, L0_conv_w_proj, L0_conv_b_proj):
    import concourse.bacc as _bacc
    from concourse.bass_utils import run_bass_kernel_spmd as _run

    def two(a):
        z = np.zeros_like(a)
        return np.concatenate([np.concatenate([a, z], 1), np.concatenate([z, a], 1)], 0)

    def everywhere(row):
        return np.broadcast_to(row, (P, row.size))

    w_qkv, w_dw = np.asarray(L0_conv_w_qkv), np.asarray(L0_conv_w_dw).reshape(QKV, TAPS)
    b_qkv, b_dw = np.asarray(L0_conv_b_qkv), np.asarray(L0_conv_b_dw)
    f = w_qkv.dtype
    one, none = np.ones(QKV, f), np.zeros((16 - TAPS - 1, QKV), f)
    bias_a = np.concatenate([np.broadcast_to(b_qkv, (TAPS, QKV)), b_dw[None], none])
    bias_d = np.concatenate([w_dw.T, one[None], none])
    per_head = np.repeat(np.asarray(L0_conv_temperature).reshape(HEADS), C // HEADS)
    arrays = {
        "x": np.asarray(x),
        "w_qkv_t": w_qkv.T,
        "w_dw_rows": everywhere(np.ascontiguousarray(w_dw.T).reshape(-1)),
        "b_qkv_rows": everywhere(b_qkv),
        "b_dw_rows": everywhere(b_dw),
        "out_scale_rows": everywhere(np.concatenate([per_head, one[:2 * C]])),
        "bias_a": np.concatenate([bias_a, bias_a]),
        "bias_d": np.concatenate([bias_d, bias_d]),
        "w_mlp_bd": two(np.asarray(L0_conv_w_mlp).T),
        "b_mlp_rows": everywhere(np.asarray(L0_conv_b_mlp)),
        "w_proj_bd": two(np.asarray(L0_conv_w_proj).T),
        "b_proj_col": np.concatenate([np.asarray(L0_conv_b_proj)] * 2).reshape(P, 1),
        **_constants(),
    }
    nc = _bacc.Bacc("TRN2", target_bir_lowering=False, num_devices=1)
    given, args = {}, []
    for name in _ORDER:
        a = np.ascontiguousarray(arrays[name])
        given[f"in_{name}"] = a
        args.append(nc.dram_tensor(f"in_{name}", a.shape, mybir.dt.from_np(a.dtype), kind="ExternalInput").ap())
    args.append(nc.dram_tensor("out_y", (B, C, H, W), F32, kind="ExternalOutput").ap())
    build(nc, *args)
    return _run(nc, [given], core_ids=[0]).results[0]["out_y"]
```

```python
from contextlib import ExitStack

import numpy as np

import concourse.bass as bass
from concourse import mybir

ALU = mybir.AluOpType
ACT = mybir.ActivationFunctionType
F32 = mybir.dt.float32
F16 = mybir.dt.float16
AX_X = mybir.AxisListType.X
ABSMAX = bass.bass_isa.ReduceOp.absmax

B, C, H, W = 4, 64, 128, 128
HEADS, WS = 4, 8
HW = WS * WS
QKV = 3 * C
P = 2 * C
PAIRS = B // 2
TAPS = 9
EPS = 1e-5

GROUPS = 4
GW = WS
STRIP = GROUPS * GW
BAND = 2 * WS
STRIPS = W // STRIP
BANDS = H // BAND
STEPS = PAIRS * BANDS * STRIPS
PAIR_STEPS = BANDS * STRIPS
PW = W + 2
PIX = PW * (H + 2)
HR, HC = BAND + 2, STRIP + 2
NP = BAND * GW
PASSES = 14
NPIX = GROUPS * P
WINDOWS = 2 * GROUPS
CHUNKS = BANDS
STAT_ROWS = 512 // W
STATS = H // STAT_ROWS
WSCALE = 1024.0
XSCALE = 64.0
BIAS_ROWS = 32
NEG = -3.0e38
TINY = 1.0e-12
SCALED = 2 * QKV
BIASES = 4 * QKV


def wait(engine, semaphore, value):
    if isinstance(value, int) and value <= 0:
        return
    engine.wait_ge(semaphore, value)


SCALES_SET = 24
MEANS_SET = SCALES_SET + 2


def build(nc, x, w_dw_rows, w_qkv_scale, biases, weights, inside_c, out):
    with ExitStack() as ctx:
        def sb(name, shape, dt=F32):
            return ctx.enter_context(nc.sbuf_tensor(name, shape, dt))

        def psum(name):
            return ctx.enter_context(nc.psum_tensor(name, [P, 512], F32))

        def sem(name):
            return ctx.enter_context(nc.semaphore(name))

        X = sb("X", [P, PAIRS * PIX])
        Xv = X[:].rearrange("p (j r c) -> p j r c", j=PAIRS, c=PW)
        Xr = X[:].rearrange("p (r c) -> p r c", c=PW)
        T = sb("T", [P, HR, HC])
        high_n = sb("high_n", [P, HR, HC], F16)
        low_n = sb("low_n", [P, HR, HC], F16)
        full, part = [P, 2, 2, GROUPS, HR * GW], [P, 2, 2, GROUPS, NP]
        high01 = sb("high01", full, F16)
        high2low0 = sb("high2low0", full, F16)
        high2low1 = sb("high2low1", full, F16)
        low2rows = sb("low2rows", part, F16)
        low2inside = sb("low2inside", part, F16)
        conv_w = sb("conv_w", [P, PASSES, QKV], F16)
        score_scale = sb("score_scale", [P, 1])
        v_scale = sb("v_scale", [P, 1])
        qkv = sb("qkv", [P, 2, GROUPS, 3, 2, C])
        scores = sb("scores", [P, WINDOWS, C])
        probs = scores
        probs_t = sb("probs_t", [P, GROUPS, 2, C])
        v_t = sb("v_t", [P, NPIX])
        gate = sb("gate", [P, NPIX])
        mixed = sb("mixed", [P, BAND, STRIP])
        neg_max = sb("neg_max", [P, WINDOWS])
        total = sb("total", [P, WINDOWS])
        inv_total = sb("inv_total", [P, WINDOWS])
        staged = sb("staged", [P, 2, BAND, W])
        consts = sb("consts", [P, 4 * P + 2 * HW + 3])
        ident, group_mean, mlp, proj = (consts[:, n * P:(n + 1) * P] for n in range(4))
        b_mlp = consts[:, 4 * P:4 * P + HW]
        other_head = consts[:, 4 * P + HW:4 * P + 2 * HW]
        b_proj = consts[:, 4 * P + 2 * HW:4 * P + 2 * HW + 1]
        split = consts[:, 4 * P + 2 * HW + 1:4 * P + 2 * HW + 3]
        inside_rc = sb("inside_rc", [P, H + W], F16)
        in_rows, in_cols = inside_rc[:, 0:H], inside_rc[:, H:H + W]
        stats = sb("stats", [P, STATS, 6])
        mean_var = sb("mean_var", [P, 2])
        small = sb("small", [P, 8])
        norm = sb("norm", [P, 2])
        scratch = staged[:].rearrange("p a b c -> p (a b c)")
        w_dw_b = scratch[:, 0:TAPS * QKV]
        w_full = scratch[:, TAPS * QKV:2 * TAPS * QKV]
        w_t = scratch[:, 2 * TAPS * QKV:2 * TAPS * QKV + QKV]
        temper = scratch[:, 2 * TAPS * QKV + QKV:2 * TAPS * QKV + 2 * QKV]
        w_max = scratch[:, 2 * TAPS * QKV + 2 * QKV:2 * TAPS * QKV + 3 * QKV]
        by_tap = "p (t o) -> p t o"
        high_w = w_dw_b[:, 0:TAPS * QKV // 2].bitcast(F16)
        low_w = w_dw_b[:, TAPS * QKV // 2:TAPS * QKV].bitcast(F16)
        bias = slice(C, C + BIAS_ROWS)
        dw_max, chan = gate[:, 0:QKV], gate[:, QKV:2 * QKV]
        spare = qkv[:, 1].rearrange("p g k t c -> p (g k t c)")
        b_qkv_b, b_dw_b, bias_a, bias_d = (spare[:, n * QKV:(n + 1) * QKV] for n in range(4))
        bias_hi = spare[bias, 4 * QKV:4 * QKV + QKV // 2].bitcast(F16)
        inv_chan = v_t[:, 0:QKV]
        bias_lo, bias_hi_f = v_t[bias, QKV:2 * QKV], scores[bias, 0:3].rearrange("p w c -> p (w c)")
        diagonal = scores[:, 4, :]

        conv_ps = [psum("conv_ps0"), psum("conv_ps1")]
        scores_ps = psum("scores_ps")
        gate_ps = psum("gate_ps")
        v_t_ps = psum("v_t_ps")
        probs_t_ps = psum("probs_t_ps")
        mix_ps = psum("mix_ps")
        proj_ps = psum("proj_ps")

        x_in = [sem(f"x_in{n}") for n in range(CHUNKS)]
        x_in_next = sem("x_in_next")
        weights_in = sem("weights_in")
        consts_in = sem("consts_in")
        w_max_ready = sem("w_max_ready")
        w_tempered = sem("w_tempered")
        w_product = sem("w_product")
        w_scaled = sem("w_scaled")
        w_high_ready = sem("w_high_ready")
        conv_w_ready = sem("conv_w_ready")
        low_w_ready = sem("low_w_ready")
        borders_clear = sem("borders_clear")
        chan_ready = sem("chan_ready")
        biases_used = sem("biases_used")
        setup = sem("setup")
        group_mean_done = sem("group_mean_done")
        centred = sem("centred")
        group_var_done = sem("group_var_done")
        var_ready = sem("var_ready")
        dev_ready = sem("dev_ready")
        norm_chain = sem("norm_chain")
        norm_ready = sem("norm_ready")
        high_ready = sem("high_ready")
        low_ready = sem("low_ready")
        operands_ready = sem("operands_ready")
        inside_ready = sem("inside_ready")
        conv_done = sem("conv_done")
        qkv_ready = sem("qkv_ready")
        gate_done = sem("gate_done")
        v_t_done = sem("v_t_done")
        scores_done = sem("scores_done")
        max_ready = sem("max_ready")
        masked = sem("masked")
        shifted = sem("shifted")
        exp_ready = sem("exp_ready")
        total_ready = sem("total_ready")
        inv_ready = sem("inv_ready")
        probs_ready = sem("probs_ready")
        probs_t_done = sem("probs_t_done")
        probs_t_ready = sem("probs_t_ready")
        v_t_ready = sem("v_t_ready")
        gate_biased = sem("gate_biased")
        gate_ready = sem("gate_ready")
        mix_done = sem("mix_done")
        mixed_ready = sem("mixed_ready")
        proj_done = sem("proj_done")
        out_ready = sem("out_ready")
        staged_free = sem("staged_free")
        stored = staged_free

        def patch(s, r0, c0, rows, cols):
            row = ((s >> 2) & (PAIRS * BANDS - 1)) * BAND + ((s >> 5) & (PAIRS - 1)) * 2
            return Xr[:, bass.ds(row + r0, rows), bass.ds((s & 3) * STRIP + c0, cols)]

        block = ctx.enter_context(nc.Block())

        @block.sync
        def _(sp):
            halves = x.rearrange("(j b) c h w -> j (b c) h w", j=PAIRS)
            rows = H // CHUNKS
            for n in range(CHUNKS):
                sp.dma_start(Xv[:, 0, 1 + n * rows:1 + (n + 1) * rows, 1:1 + W],
                             halves[0, :, n * rows:(n + 1) * rows, :]).then_inc(x_in[n], 16)
            sp.wait_ge(consts_in, 16 * 2)
            for n in range(CHUNKS):
                sp.dma_start(Xv[:, 1, 1 + n * rows:1 + (n + 1) * rows, 1:1 + W],
                             halves[1, :, n * rows:(n + 1) * rows, :]).then_inc(x_in_next, 16)
            bands = out.rearrange("(j b) c h w -> j (b c) h w", j=PAIRS)
            for j in range(PAIRS):
                with sp.Fori(0, BANDS // 2) as i:
                    for k in range(2):
                        sp.wait_ge(out_ready, (i * 2 + (j * BANDS + k + 1)) * STRIPS)
                        sp.wait_ge(stored, (i * 2 + (j * BANDS + k + 2)) * 16)
                        sp.dma_start(bands[j, :, bass.ds((i * 2 + k) * BAND, BAND), :],
                                     staged[:, k]).then_inc(stored, 16)
            sp.wait_ge(stored, 16 * (2 + PAIRS * BANDS))

        @block.gpsimd
        def _(pool):
            nc.gpsimd.memset(Xv[:, :, 0:H + 2:H + 1, :], 0.0)
            nc.gpsimd.memset(Xv[:, :, 1:H + 1, 0:PW:PW - 1], 0.0).then_inc(borders_clear, 1)
            nc.gpsimd.memset(small[:, 6:7], 0.0).then_inc(staged_free, 32)
            pool.wait_ge(weights_in, 16 * 3)
            nc.gpsimd.tensor_tensor(w_t, w_t, temper, ALU.mult).then_inc(w_tempered, 1)
            pool.wait_ge(w_tempered, 1)
            nc.gpsimd.partition_all_reduce(w_max, w_t, P, ABSMAX).then_inc(w_max_ready, 1)
            over = [P, TAPS, QKV]
            wf = w_full.rearrange(by_tap, t=TAPS)
            nc.gpsimd.tensor_tensor(wf, w_dw_b.rearrange(by_tap, t=TAPS), w_t.unsqueeze(1).to_broadcast(over),
                                    ALU.mult).then_inc(w_product, 1)
            pool.wait_ge(w_product, 1)
            pool.wait_ge(chan_ready, 1)
            nc.gpsimd.tensor_tensor(wf, wf, inv_chan.unsqueeze(1).to_broadcast(over), ALU.mult).then_inc(w_scaled, 1)
            pool.wait_ge(biases_used, 1)
            pool.wait_ge(w_scaled, 1)
            pool.wait_ge(consts_in, 16 * 2)

            def inside(s, k):
                wait(pool, conv_done, (s - 1) * GROUPS)
                r = in_rows[bias, bass.ds(((s >> 2) & (BANDS - 1)) * BAND, BAND)]
                c = in_cols[bias, bass.ds((s & (STRIPS - 1)) * STRIP, STRIP)].rearrange("p (g c) -> p g c", c=GW)
                over = [BIAS_ROWS, GROUPS, BAND, GW]
                for t in range(2):
                    last = nc.gpsimd.tensor_tensor(
                        low2inside[bias, k, t].rearrange("p g (r c) -> p g r c", c=GW),
                        r.unsqueeze(1).unsqueeze(3).to_broadcast(over), c.unsqueeze(2).to_broadcast(over), ALU.mult)
                last.then_inc(inside_ready, 1)

            inside(0, 0)
            inside(1, 1)
            with pool.Fori(1, STEPS // 2) as i:
                for k in range(2):
                    inside(i * 2 + k, k)

        @block.scalar
        def _(act):
            act.dma_start(scratch[:, 2 * TAPS * QKV:2 * TAPS * QKV + SCALED], w_qkv_scale).then_inc(weights_in, 16)
            act.dma_start(w_dw_b, w_dw_rows).then_inc(weights_in, 16)
            act.dma_start(spare[:, 0:BIASES], biases).then_inc(weights_in, 16)
            act.dma_start(consts[:], weights).then_inc(consts_in, 16)
            act.dma_start(inside_rc[:], inside_c).then_inc(consts_in, 16)

            def conv_weights():
                act.wait_ge(w_scaled, 1)
                act.wait_ge(chan_ready, 1)
                nc.scalar.activation(high_w, w_full, ACT.Copy).then_inc(w_high_ready, 1)
                act.wait_ge(w_high_ready, 1)
                hw, lw = (w.rearrange("p (y x o) -> p y x o", y=3, x=3) for w in (high_w, low_w))
                up, down = slice(0, C), slice(C, P)
                for first, half, of, col in ((0, up, hw, 0), (0, down, hw, 1), (6, up, hw, 2), (6, down, hw, 0),
                                             (9, down, hw, 1), (3, up, lw, 0), (3, down, lw, 1), (9, up, lw, 2)):
                    if of is lw:
                        act.wait_ge(low_w_ready, 1)
                    nc.scalar.activation(conv_w[half, first:first + 3, :], of[half, :, col, :], ACT.Copy)
                nc.scalar.activation(conv_w[up, 12, :], hw[up, 0, 2, :], ACT.Copy)
                nc.scalar.activation(conv_w[down, 12, :], hw[down, 1, 2, :], ACT.Copy)
                nc.scalar.activation(conv_w[up, 13, :], hw[up, 2, 2, :], ACT.Copy).then_inc(conv_w_ready, 1)

            def deviation(n):
                act.wait_ge(var_ready, n)
                nc.scalar.activation(small[:, 3:4], small[:, 2:3], ACT.Sqrt).then_inc(dev_ready, 1)

            def high(s):
                act.wait_ge(norm_ready, s + 1)
                wait(act, operands_ready, s)
                nc.scalar.activation(high_n[:], T[:], ACT.Copy).then_inc(high_ready, 1)

            def evacuate(s, k, g):
                act.wait_ge(conv_done, s * GROUPS + (g + 1))
                wait(act, v_t_done, s - 1)
                nc.scalar.activation(qkv[:, k, g].rearrange("p k t c -> p t k c"),
                                     conv_ps[g % 2][:, 0:2 * QKV].rearrange("p (t k c) -> p t k c", t=2, k=3),
                                     ACT.Copy).then_inc(qkv_ready, 1)

            def v_up(s):
                act.wait_ge(v_t_done, s)
                wait(act, mix_done, s - 1)
                nc.scalar.activation(v_t[:], v_t_ps[:], ACT.Identity, scale=v_scale[:, 0:1]).then_inc(v_t_ready, 1)

            def exponent(s):
                act.wait_ge(shifted, s)
                nc.scalar.activation(probs[:], scores[:], ACT.Exp, scale=score_scale[:, 0:1]).then_inc(exp_ready, 1)

            def gelu(s):
                act.wait_ge(gate_biased, s)
                nc.scalar.activation(gate[:], gate[:], ACT.Gelu).then_inc(gate_ready, 1)
                nc.scalar.activation(small[:, 7:8], small[:, 6:7], ACT.Exp)

            def probs_up(s):
                act.wait_ge(probs_t_done, s)
                wait(act, mix_done, s - 1)
                nc.scalar.activation(probs_t[:], probs_t_ps[:].rearrange("p (g u c) -> p g u c", g=GROUPS, u=2),
                                     ACT.Copy).then_inc(probs_t_ready, 1)

            def step(s, k, conv=True, prepare=True, attend=True, new_pair=0):
                if conv:
                    evacuate(s, k, 0)
                if attend:
                    exponent(s)
                if conv:
                    evacuate(s, k, 1)
                if attend:
                    v_up(s)
                if conv:
                    evacuate(s, k, 2)
                if attend:
                    probs_up(s)
                if conv:
                    evacuate(s, k, 3)
                if new_pair:
                    deviation(new_pair)
                if prepare:
                    high(s + 2)
                if attend:
                    gelu(s)

            conv_weights()
            deviation(1)
            high(0)
            high(1)
            step(0, 0, attend=False)
            act.wait_ge(setup, SCALES_SET)
            step(1, 1)
            with act.Fori(1, (PAIR_STEPS - 2) // 2) as i:
                for k in range(2):
                    step(i * 2 + k, k)
            step(PAIR_STEPS - 2, 0, new_pair=2)
            step(PAIR_STEPS - 1, 1)
            with act.Fori(PAIR_STEPS // 2, STEPS // 2 - 1) as i:
                for k in range(2):
                    step(i * 2 + k, k)
            step(STEPS - 2, 0, prepare=False)
            step(STEPS - 1, 1, prepare=False)
            step(STEPS, 0, conv=False, prepare=False)

        @block.vector
        def _(dve):
            count = [0]

            def link(ins):
                count[0] += 1
                ins.then_inc(setup, 1)
                dve.wait_ge(setup, count[0])

            def statistics(pair, n):
                rows = Xr[:, bass.ds(n * STAT_ROWS + (pair * (H + 2) + 1), STAT_ROWS), 1:1 + W]
                return nc.vector.bn_stats(stats[:, bass.ds(n, 1), :], rows)

            def normaliser(pair):
                c0 = pair * 7
                dve.wait_ge(borders_clear, 1)
                link(nc.vector.bn_aggr(mean_var[:], stats[:].rearrange("p n k -> p (n k)")))
                dve.wait_ge(group_mean_done, pair + 1)
                if pair:
                    dve.wait_ge(norm_ready, PAIR_STEPS)
                nc.vector.tensor_copy(norm[:, 0:1], proj_ps[:, 0:1]).then_inc(norm_chain, 1)
                dve.wait_ge(norm_chain, c0 + 1)
                nc.vector.tensor_tensor(small[:, 0:1], mean_var[:, 0:1], norm[:, 0:1],
                                        ALU.subtract).then_inc(norm_chain, 1)
                dve.wait_ge(norm_chain, c0 + 2)
                nc.vector.scalar_tensor_tensor(small[:, 1:2], small[:, 0:1], small[:, 0:1], mean_var[:, 1:2],
                                               op0=ALU.mult, op1=ALU.add).then_inc(centred, 1)
                dve.wait_ge(group_var_done, pair + 1)
                nc.vector.tensor_scalar(small[:, 2:3], proj_ps[:, 1:2], EPS, None, ALU.add).then_inc(var_ready, 1)
                dve.wait_ge(dev_ready, pair + 1)
                nc.vector.reciprocal(small[:, 4:5], small[:, 3:4]).then_inc(norm_chain, 1)
                dve.wait_ge(norm_chain, c0 + 3)
                nc.vector.scalar_tensor_tensor(small[:, 5:6], small[:, 4:5], small[:, 4:5], small[:, 2:3],
                                               op0=ALU.mult, op1=ALU.mult).then_inc(norm_chain, 1)
                dve.wait_ge(norm_chain, c0 + 4)
                nc.vector.tensor_scalar(small[:, 5:6], small[:, 5:6], -0.5 * XSCALE, 1.5 * XSCALE,
                                        ALU.mult, ALU.add).then_inc(norm_chain, 1)
                dve.wait_ge(norm_chain, c0 + 5)
                nc.vector.tensor_tensor(norm[:, 1:2], small[:, 4:5], small[:, 5:6], ALU.mult).then_inc(norm_chain, 1)
                for edge in (Xv[:, pair, 0:H + 2:H + 1, :], Xv[:, pair, 1:H + 1, 0:PW:PW - 1]):
                    last = nc.vector.tensor_scalar(edge, edge, norm[:, 0:1], None, ALU.add)
                last.then_inc(norm_chain, 1)
                dve.wait_ge(norm_chain, c0 + 7)

            def normalise(s):
                wait(dve, high_ready, s)
                wait(dve, operands_ready, s)
                nc.vector.tensor_scalar(T[:], patch(s, 0, 0, HR, HC), norm[:, 0:1], norm[:, 1:2],
                                        ALU.subtract, ALU.mult).then_inc(norm_ready, 1)

            def low(s):
                dve.wait_ge(high_ready, s + 1)
                nc.vector.tensor_tensor(low_n[:], T[:], high_n[:], ALU.subtract).then_inc(low_ready, 1)

            def operands(s, k, t):
                dve.wait_ge(low_ready, s + 1)
                wait(dve, conv_done, (s - 1) * GROUPS)
                upper, lower = slice(0, C), slice(C, P)
                image = slice(t * C, t * C + C)
                for to, half, of, col, row in (
                        (high01, upper, high_n, 0, 0), (high01, lower, high_n, 1, 0),
                        (high2low0, upper, high_n, 2, 0), (high2low0, lower, low_n, 0, 0),
                        (high2low1, upper, high_n, 2, 0), (high2low1, lower, low_n, 1, 0),
                        (low2rows, upper, low_n, 2, 0), (low2rows, lower, low_n, 2, 1),
                        (low2inside, upper, low_n, 2, 2)):
                    to = to[half, k, t].rearrange("p g (r c) -> p g r c", c=GW)
                    of = of[image, row:row + to.shape[2], col:col + STRIP]
                    last = nc.vector.tensor_copy(to, of.rearrange("p r (g c) -> p g r c", c=GW))
                if t == 1:
                    last.then_inc(operands_ready, 1)

            def mix(s):
                dve.wait_ge(mix_done, s - 1)
                dve.wait_ge(gate_ready, s - 1)
                wait(dve, proj_done, s - 2)
                nc.vector.tensor_tensor(
                    mixed[:].rearrange("p r (g c) -> p g r c", g=GROUPS),
                    mix_ps[:].rearrange("p (g r c) -> p g r c", g=GROUPS, c=GW),
                    gate[:].rearrange("p (g r c) -> p g r c", g=GROUPS, c=GW), ALU.mult).then_inc(mixed_ready, 1)

            def scores_up(s):
                dve.wait_ge(scores_done, s)
                wait(dve, probs_t_done, s - 1)
                over = [P, WINDOWS, C]
                nc.vector.tensor_tensor(scores[:], scores_ps[:].rearrange("p (w c) -> p w c", c=C),
                                        other_head.unsqueeze(1).to_broadcast(over), ALU.add).then_inc(masked, 1)
                dve.wait_ge(masked, s)
                nc.vector.tensor_reduce(neg_max[:], scores[:], AX_X, ALU.max, negate=True).then_inc(max_ready, 1)
                dve.wait_ge(max_ready, s)
                nc.vector.tensor_tensor(scores[:], scores[:], neg_max[:].unsqueeze(2).to_broadcast(over),
                                        ALU.add).then_inc(shifted, 1)

            def gate_up(s):
                dve.wait_ge(gate_done, s)
                wait(dve, mixed_ready, s - 1)
                nc.vector.scalar_tensor_tensor(
                    gate[:].rearrange("p (w y) -> p w y", y=HW), gate_ps[:].rearrange("p (w y) -> p w y", y=HW),
                    v_scale[:, 0:1], b_mlp.unsqueeze(1).to_broadcast([P, WINDOWS, HW]), op0=ALU.mult,
                    op1=ALU.add).then_inc(gate_biased, 1)

            def divide(s):
                dve.wait_ge(exp_ready, s)
                nc.vector.tensor_reduce(total[:], probs[:], AX_X, ALU.add).then_inc(total_ready, 1)
                dve.wait_ge(total_ready, s)
                nc.vector.reciprocal(inv_total[:], total[:]).then_inc(inv_ready, 1)
                dve.wait_ge(inv_ready, s)
                nc.vector.tensor_tensor(probs[:], probs[:],
                                        inv_total[:].unsqueeze(2).to_broadcast([P, WINDOWS, C]),
                                        ALU.mult).then_inc(probs_ready, 1)

            def residual(s):
                r = s - 2
                dve.wait_ge(proj_done, s - 1)
                dve.wait_ge(staged_free, ((r >> 2) + 1) * 16)
                to = staged[:].rearrange("p a r w -> p (a r) w")
                to = to[:, bass.ds(((r >> 2) & 1) * BAND, BAND), bass.ds((r & 3) * STRIP, STRIP)]
                nc.vector.scalar_tensor_tensor(to, proj_ps[:].rearrange("p (r c) -> p r c", c=STRIP), b_proj,
                                               patch(r, 1, 1, BAND, STRIP), op0=ALU.add,
                                               op1=ALU.add).then_inc(out_ready, 1)

            def step(s, k, prepare=True, attend=True, finish=True, ahead=True, more=()):
                if prepare:
                    low(s + 1)
                    operands(s + 1, 1 - k, 0)
                if finish:
                    mix(s)
                if attend:
                    scores_up(s)
                    gate_up(s)
                    divide(s)
                if prepare:
                    operands(s + 1, 1 - k, 1)
                for pair, n in more:
                    statistics(pair, n)
                if ahead:
                    normalise(s + 2)
                if finish:
                    residual(s)

            def scales():
                link(nc.vector.tensor_reduce(dw_max, w_dw_b.rearrange("p (t o) -> p o t", t=TAPS), AX_X, ALU.max,
                                             apply_absolute_value=True))
                for b in (b_qkv_b, b_dw_b):
                    link(nc.vector.tensor_tensor(b, b, temper, ALU.mult))
                for b in (b_qkv_b, b_dw_b):
                    link(nc.vector.scalar_tensor_tensor(b, b, -1.0, b, op0=ALU.mult, op1=ALU.max))
                dve.wait_ge(w_max_ready, 1)
                link(nc.vector.tensor_tensor(chan, w_max, b_qkv_b, ALU.max))
                link(nc.vector.tensor_tensor(chan, chan, dw_max, ALU.mult))
                link(nc.vector.tensor_tensor(chan, chan, b_dw_b, ALU.max))
                link(nc.vector.tensor_scalar(chan, chan, TINY, None, ALU.max))
                link(nc.vector.tensor_reduce(small[:, 5:6], chan[:, C:2 * C], AX_X, ALU.max))
                link(nc.vector.tensor_scalar(chan[:, C:2 * C], chan[:, C:2 * C], 0.0, small[:, 5:6], ALU.mult, ALU.add))
                link(nc.vector.reciprocal(inv_chan, chan))
                dve.wait_ge(w_product, 1)
                nc.vector.tensor_scalar(inv_chan, inv_chan, WSCALE, None, ALU.mult).then_inc(chan_ready, 1)

            def scale_columns():
                for part, column in ((0, score_scale), (2, v_scale)):
                    for half in (slice(0, C), slice(C, P)):
                        last = nc.vector.tensor_tensor(diagonal[half], chan[half, part * C:(part + 1) * C],
                                                       ident[half, half], ALU.mult)
                    link(last)
                    link(nc.vector.tensor_reduce(column[:], diagonal, AX_X, ALU.add))
                unscale = 1.0 / (WSCALE * XSCALE)
                link(nc.vector.tensor_scalar(v_scale[:], v_scale[:], unscale, None, ALU.mult))
                link(nc.vector.tensor_scalar(score_scale[:], score_scale[:], unscale * unscale, chan[:, C:C + 1],
                                             ALU.mult, ALU.mult))

            def bias_weights():
                dve.wait_ge(chan_ready, 1)
                a = bias_a[bias]
                link(nc.vector.tensor_tensor(a, a, bias_d[bias], ALU.mult))
                link(nc.vector.tensor_tensor(a, a, temper[bias], ALU.mult))
                link(nc.vector.tensor_tensor(a, a, inv_chan[bias], ALU.mult))
                link(nc.vector.tensor_copy(bias_hi, a))
                link(nc.vector.tensor_tensor(bias_lo, a, bias_hi, ALU.subtract))
                link(nc.vector.tensor_scalar(bias_hi_f, bias_hi, split[bias, 0:1], None, ALU.mult))
                nc.vector.scalar_tensor_tensor(conv_w[bias, 13, :], bias_lo, split[bias, 1:2], bias_hi_f,
                                               op0=ALU.mult, op1=ALU.add).then_inc(biases_used, 1)
                dve.wait_ge(biases_used, 1)

            def low_weights():
                dve.wait_ge(w_high_ready, 1)
                nc.vector.tensor_tensor(low_w, w_full, high_w, ALU.subtract).then_inc(low_w_ready, 1)
                dve.wait_ge(low_w_ready, 1)

            each = STATS // CHUNKS
            for n in range(CHUNKS):
                dve.wait_ge(x_in[n], 16)
                for m in range(each):
                    last = statistics(0, n * each + m)
                if n == 1:
                    dve.wait_ge(weights_in, 16 * 3)
                    scales()
                if n == 3:
                    dve.wait_ge(consts_in, 16 * 2)
                    bias_weights()
                    scale_columns()
                if n == 6:
                    low_weights()
            link(last)
            assert count[0] == SCALES_SET + 1, count
            normaliser(0)
            assert count[0] == MEANS_SET, count
            normalise(0)
            low(0)
            operands(0, 0, 0)
            operands(0, 0, 1)
            normalise(1)
            step(0, 0, attend=False, finish=False)
            step(1, 1, finish=False)
            stat_from = PAIR_STEPS - 2 - STATS // 2
            with dve.Fori(1, stat_from // 2) as i:
                for k in range(2):
                    step(i * 2 + k, k)
            dve.wait_ge(x_in_next, 16 * CHUNKS)
            with dve.Fori(stat_from // 2, (PAIR_STEPS - 2) // 2) as i:
                for k in range(2):
                    step(i * 2 + k, k, more=[(1, i * 4 + (2 * k + m - 2 * stat_from)) for m in range(2)])
            step(PAIR_STEPS - 2, 0, ahead=False)
            normaliser(1)
            normalise(PAIR_STEPS)
            step(PAIR_STEPS - 1, 1)
            with dve.Fori(PAIR_STEPS // 2, STEPS // 2 - 1) as i:
                for k in range(2):
                    step(i * 2 + k, k)
            step(STEPS - 2, 0, ahead=False)
            step(STEPS - 1, 1, prepare=False, ahead=False)
            step(STEPS, 0, prepare=False, ahead=False)
            step(STEPS + 1, 1, prepare=False, attend=False, ahead=False)

        @block.tensor
        def _(pe):
            def group_stats(n):
                pe.wait_ge(setup, MEANS_SET + n - 1)
                wait(pe, out_ready, 0 if n == 1 else PAIR_STEPS - 3)
                nc.tensor.matmul(proj_ps[:, 0:1], group_mean, mean_var[:, 0:1], start=True,
                                 stop=True).then_inc(group_mean_done, 1)
                pe.wait_ge(centred, n)
                nc.tensor.matmul(proj_ps[:, 1:2], group_mean, small[:, 1:2], start=True,
                                 stop=True).then_inc(group_var_done, 1)

            def conv(s, k, g):
                if g == 0:
                    pe.wait_ge(operands_ready, s + 1)
                    pe.wait_ge(inside_ready, s + 1)
                wait(pe, qkv_ready, s * GROUPS + (g - 1))
                for t in range(2):
                    def rows(tensor, y=0, p=P):
                        return tensor[0:p, k, t, g, y * GW:y * GW + NP]
                    passes = [rows(high01, y) for y in range(3)] * 2
                    passes += [rows(high2low0, y) for y in range(3)] + [rows(high2low1, y) for y in range(3)]
                    passes += [rows(low2rows), rows(low2inside, p=C + BIAS_ROWS)]
                    for n, pixels in enumerate(passes):
                        last = nc.tensor.matmul(conv_ps[g % 2][:, t * QKV:(t + 1) * QKV], pixels,
                                                conv_w[0:pixels.shape[0], n, :],
                                                start=(n == 0), stop=(n == len(passes) - 1))
                last.then_inc(conv_done, 1)

            def attend(s, k):
                pe.wait_ge(qkv_ready, s * GROUPS)
                wait(pe, masked, s - 1)
                wait(pe, gate_biased, s - 1)
                for g in range(GROUPS):
                    v = qkv[:, k, g, 2].rearrange("p t c -> p (t c)")
                    last = nc.tensor.matmul(gate_ps[:, g * P:(g + 1) * P], v, mlp, start=True, stop=True)
                last.then_inc(gate_done, 1)
                for g in range(GROUPS):
                    for t in range(2):
                        for u in range(2):
                            h = slice(u * HW, (u + 1) * HW)
                            last = nc.tensor.matmul(
                                scores_ps[u * C:(u + 1) * C, (2 * g + t) * C:(2 * g + t + 1) * C],
                                qkv[h, k, g, 0, t, :], qkv[h, k, g, 1, t, :], start=True, stop=True)
                last.then_inc(scores_done, 1)
                wait(pe, v_t_ready, s - 1)
                for g in range(GROUPS):
                    v = qkv[:, k, g, 2].rearrange("p t c -> p (t c)")
                    last = nc.tensor.transpose(v_t_ps[:, g * P:(g + 1) * P], v, ident)
                last.then_inc(v_t_done, 1)

            def turn_probs(s):
                pe.wait_ge(probs_ready, s)
                wait(pe, probs_t_ready, s - 1)
                for g in range(GROUPS):
                    last = nc.tensor.transpose(probs_t_ps[:, g * P:(g + 1) * P],
                                               probs[:, 2 * g:2 * g + 2, :].rearrange("p t c -> p (t c)"), ident)
                last.then_inc(probs_t_done, 1)

            def wait_for_probs(s):
                pe.wait_ge(probs_t_ready, s)
                pe.wait_ge(v_t_ready, s)
                wait(pe, mixed_ready, s - 1)

            def apply_probs(s):
                for g in range(GROUPS):
                    for u in range(2):
                        at = slice(g * P + u * HW, g * P + (u + 1) * HW)
                        for t in range(2):
                            h = slice(t * C, (t + 1) * C)
                            last = nc.tensor.matmul(mix_ps[h, at], probs_t[h, g, u, :], v_t[h, at],
                                                    start=True, stop=True)
                last.then_inc(mix_done, 1)

            def project(s):
                pe.wait_ge(mixed_ready, s - 1)
                wait(pe, out_ready, s - 2)
                nc.tensor.matmul(proj_ps[:], proj, mixed[:].rearrange("p r c -> p (r c)"), start=True,
                                 stop=True).then_inc(proj_done, 1)

            def step(s, k, convolve=True, attention=True, finish=True):
                if convolve:
                    conv(s, k, 0)
                if attention:
                    attend(s, 1 - k)
                if convolve:
                    conv(s, k, 1)
                if convolve:
                    conv(s, k, 2)
                if attention:
                    turn_probs(s)
                if convolve:
                    conv(s, k, 3)
                if attention:
                    wait_for_probs(s)
                if finish:
                    project(s)
                if attention:
                    apply_probs(s)

            pe.wait_ge(consts_in, 16 * 2)
            group_stats(1)
            pe.wait_ge(conv_w_ready, 1)
            pe.wait_ge(biases_used, 1)
            step(0, 0, attention=False, finish=False)
            step(1, 1, finish=False)
            with pe.Fori(1, (PAIR_STEPS - 2) // 2) as i:
                for k in range(2):
                    step(i * 2 + k, k)
            step(PAIR_STEPS - 2, 0)
            group_stats(2)
            step(PAIR_STEPS - 1, 1)
            with pe.Fori(PAIR_STEPS // 2, STEPS // 2) as i:
                for k in range(2):
                    step(i * 2 + k, k)
            step(STEPS, 0, convolve=False)
            step(STEPS + 1, 1, convolve=False, attention=False)


_ORDER = ("x", "w_dw_rows", "w_qkv_scale", "biases", "weights", "inside")


def _inside():
    tap = np.arange(16)
    dy, dx = tap // 3 - 1, tap % 3 - 1
    dy[TAPS:], dx[TAPS:] = 0, 0
    at = np.arange(H)
    rows = ((at + dy[:, None] >= 0) & (at + dy[:, None] < H)) * XSCALE
    cols = ((at + dx[:, None] >= 0) & (at + dx[:, None] < W)) * 1.0
    rows[TAPS + 1:] = 0
    return np.tile(np.concatenate([rows, cols], 1), (P // 16, 1)).astype(np.float16)


def _other_head():
    head = np.arange(P) % C // (C // HEADS)
    return np.where(head[:, None] == head[None, :C], 0.0, NEG).astype(np.float32)


def kernel(x, L0_conv_w_qkv, L0_conv_b_qkv, L0_conv_w_dw, L0_conv_b_dw, L0_conv_temperature, L0_conv_w_mlp,
           L0_conv_b_mlp, L0_conv_w_proj, L0_conv_b_proj):
    import concourse.bacc as _bacc
    from concourse.bass_utils import run_bass_kernel_spmd as _run

    def two(a):
        z = np.zeros_like(a)
        return np.concatenate([np.concatenate([a, z], 1), np.concatenate([z, a], 1)], 0)

    def everywhere(row):
        return np.broadcast_to(row, (P, row.size))

    w_qkv, w_dw = np.asarray(L0_conv_w_qkv), np.asarray(L0_conv_w_dw).reshape(QKV, TAPS)
    b_qkv, b_dw = np.asarray(L0_conv_b_qkv), np.asarray(L0_conv_b_dw)
    f = w_qkv.dtype
    one, none = np.ones(QKV, f), np.zeros((16 - TAPS - 1, QKV), f)
    bias_a = np.concatenate([np.broadcast_to(b_qkv, (TAPS, QKV)), b_dw[None], none] * (P // 16))
    bias_d = np.concatenate([w_dw.T, one[None], none] * (P // 16))
    per_head = np.repeat(np.asarray(L0_conv_temperature).reshape(HEADS), C // HEADS)
    temper = np.concatenate([per_head, one[:2 * C]])
    chan = np.arange(P)
    group = (0.5 * (chan[:, None] // 2 == chan[None, :] // 2)).astype(f)
    arrays = {
        "x": np.asarray(x),
        "w_dw_rows": everywhere(np.ascontiguousarray(w_dw.T).reshape(-1)),
        "w_qkv_scale": np.concatenate([np.concatenate([w_qkv.T] * 2), everywhere(temper)], 1),
        "biases": np.concatenate([everywhere(b_qkv), everywhere(b_dw), bias_a, bias_d], 1),
        "weights": np.concatenate([
            np.eye(P, dtype=f), group, two(np.asarray(L0_conv_w_mlp).T), two(np.asarray(L0_conv_w_proj).T),
            everywhere(np.asarray(L0_conv_b_mlp)), _other_head(), np.concatenate([np.asarray(L0_conv_b_proj)] * 2).reshape(P, 1),
            np.tile(np.repeat(np.eye(2, dtype=f), 16, axis=0), (P // 32, 1))], 1),
        "inside": _inside(),
    }
    nc = _bacc.Bacc("TRN2", target_bir_lowering=False, num_devices=1)
    given, args = {}, []
    for name in _ORDER:
        a = np.ascontiguousarray(arrays[name])
        given[f"in_{name}"] = a
        args.append(nc.dram_tensor(f"in_{name}", a.shape, mybir.dt.from_np(a.dtype), kind="ExternalInput").ap())
    args.append(nc.dram_tensor("out_y", (B, C, H, W), F32, kind="ExternalOutput").ap())
    build(nc, *args)
    return _run(nc, [given], core_ids=[0]).results[0]["out_y"]
```

```python
from contextlib import ExitStack

import numpy as np

import concourse.bass as bass
from concourse import mybir

ALU = mybir.AluOpType
ACT = mybir.ActivationFunctionType
F32 = mybir.dt.float32
F16 = mybir.dt.float16
AX_X = mybir.AxisListType.X
ABSMAX = bass.bass_isa.ReduceOp.absmax

B, C, H, W = 4, 64, 128, 128
HEADS, WS = 4, 8
HW = WS * WS
QKV = 3 * C
P = 2 * C
PAIRS = B // 2
TAPS = 9
EPS = 1e-5

GROUPS = 4
GW = WS
STRIP = GROUPS * GW
BAND = 2 * WS
STRIPS = W // STRIP
BANDS = H // BAND
STEPS = PAIRS * BANDS * STRIPS
PAIR_STEPS = BANDS * STRIPS
PW = W + 2
PIX = PW * (H + 2)
HR, HC = BAND + 2, STRIP + 2
NP = BAND * GW
PASSES = 14
NPIX = GROUPS * P
WINDOWS = 2 * GROUPS
CHUNKS = BANDS
CHUNK_ROWS = [H // CHUNKS] * (CHUNKS - 1) + [H // CHUNKS // 2] * 2
STAT_ROWS = 512 // W
STATS = H // STAT_ROWS
WSCALE = 1024.0
XSCALE = 64.0
BIAS_ROWS = 32
NEG = -3.0e38
TINY = 1.0e-12
SCALED = 2 * QKV
WARM_START, WARM_END = 36, 50
NORM_LINKS = 7
MEANS_SET = 11
SCALES_SET = MEANS_SET + 6
BAND_SHIFT, PAIR_SHIFT = 2, 5
assert (STRIPS, PAIR_STEPS) == (1 << BAND_SHIFT, 1 << PAIR_SHIFT)


def wait(engine, semaphore, value):
    if isinstance(value, int) and value <= 0:
        return
    engine.wait_ge(semaphore, value)


def build(nc, x, w_dw_rows, w_qkv_scale, biases, bias_rows, weights, inside_c, out):
    with ExitStack() as ctx:
        def sb(name, shape, dt=F32):
            return ctx.enter_context(nc.sbuf_tensor(name, shape, dt))

        def psum(name):
            return ctx.enter_context(nc.psum_tensor(name, [P, 512], F32))

        def sem(name):
            return ctx.enter_context(nc.semaphore(name))

        X = sb("X", [P, PAIRS * PIX])
        Xv = X[:].rearrange("p (j r c) -> p j r c", j=PAIRS, c=PW)
        Xr = X[:].rearrange("p (r c) -> p r c", c=PW)
        T = sb("T", [P, HR, HC])
        high_n = sb("high_n", [P, HR, HC], F16)
        low_n = sb("low_n", [P, HR, HC], F16)
        full, part = [P, 2, 2, GROUPS, HR * GW], [P, 2, 2, GROUPS, NP]
        high01 = sb("high01", full, F16)
        high2low0 = sb("high2low0", full, F16)
        high2low1 = sb("high2low1", full, F16)
        low2rows = sb("low2rows", part, F16)
        low2inside = sb("low2inside", part, F16)
        conv_w = sb("conv_w", [P, PASSES, QKV], F16)
        score_scale = sb("score_scale", [P, 1])
        v_scale = sb("v_scale", [P, 1])
        qkv = sb("qkv", [P, 2, GROUPS, 3, 2, C])
        scores = sb("scores", [P, WINDOWS, C])
        probs_t = sb("probs_t", [P, GROUPS, 2, C])
        v_t = sb("v_t", [P, NPIX])
        gate = sb("gate", [P, NPIX])
        mixed = sb("mixed", [P, BAND, STRIP])
        neg_max = sb("neg_max", [P, WINDOWS])
        total = sb("total", [P, WINDOWS])
        inv_total = sb("inv_total", [P, WINDOWS])
        staged = sb("staged", [P, 2, BAND, W])
        consts = sb("consts", [P, 4 * P + 2 * HW + 3])
        ident, group_mean, mlp, proj = (consts[:, n * P:(n + 1) * P] for n in range(4))
        b_mlp = consts[:, 4 * P:4 * P + HW]
        other_head = consts[:, 4 * P + HW:4 * P + 2 * HW]
        b_proj = consts[:, 4 * P + 2 * HW:4 * P + 2 * HW + 1]
        split = consts[:, 4 * P + 2 * HW + 1:4 * P + 2 * HW + 3]
        inside_rc = sb("inside_rc", [P, H + W], F16)
        in_rows, in_cols = inside_rc[:, 0:H], inside_rc[:, H:H + W]
        stats = sb("stats", [P, STATS, 6])
        mean_var = sb("mean_var", [P, 2])
        small = sb("small", [P, 8])
        norm = sb("norm", [P, 2])
        scratch = staged[:].rearrange("p a b c -> p (a b c)")
        w_dw_b = scratch[:, 0:TAPS * QKV]
        w_full = scratch[:, TAPS * QKV:2 * TAPS * QKV]
        w_t = scratch[:, 2 * TAPS * QKV:2 * TAPS * QKV + QKV]
        temper = scratch[:, 2 * TAPS * QKV + QKV:2 * TAPS * QKV + 2 * QKV]
        w_max = scratch[:, 2 * TAPS * QKV + 2 * QKV:2 * TAPS * QKV + 3 * QKV]
        by_tap = "p (t o) -> p t o"
        high_w = w_dw_b[:, 0:TAPS * QKV // 2].bitcast(F16)
        low_w = w_dw_b[:, TAPS * QKV // 2:TAPS * QKV].bitcast(F16)
        bias = slice(C, C + BIAS_ROWS)
        dw_max, chan = gate[:, 0:QKV], gate[:, QKV:2 * QKV]
        spare = qkv[:, 1].rearrange("p g k t c -> p (g k t c)")
        b_both = spare[:, 0:2 * QKV]
        b_qkv_b, b_dw_b, bias_a, bias_d = (spare[:, n * QKV:(n + 1) * QKV] for n in range(4))
        bias_hi = spare[bias, 4 * QKV:4 * QKV + QKV // 2].bitcast(F16)
        inv_chan = v_t[:, 0:QKV]
        bias_lo, bias_hi_f = v_t[bias, QKV:2 * QKV], scores[bias, 0:3].rearrange("p w c -> p (w c)")
        diagonal = scores[:, 4, :]

        conv_ps = [psum("conv_ps0"), psum("conv_ps1")]
        scores_ps = psum("scores_ps")
        gate_ps = psum("gate_ps")
        v_t_ps = psum("v_t_ps")
        mix_ps = psum("mix_ps")
        proj_ps = psum("proj_ps")

        x_in = [sem(f"x_in{n}") for n in range(len(CHUNK_ROWS))]
        x_in_next = sem("x_in_next")
        w_dw_in = sem("w_dw_in")
        weights_in = sem("weights_in")
        consts_in = sem("consts_in")
        w_max_ready = sem("w_max_ready")
        w_tempered = sem("w_tempered")
        w_product = sem("w_product")
        w_scaled = sem("w_scaled")
        w_high_ready = sem("w_high_ready")
        conv_w_ready = sem("conv_w_ready")
        low_w_ready = sem("low_w_ready")
        borders_clear = sem("borders_clear")
        chan_ready = sem("chan_ready")
        bias_chain = sem("bias_chain")
        biases_used = sem("biases_used")
        setup = sem("setup")
        group_mean_done = sem("group_mean_done")
        centred = sem("centred")
        group_var_done = sem("group_var_done")
        var_ready = sem("var_ready")
        dev_ready = sem("dev_ready")
        norm_chain = sem("norm_chain")
        norm_ready = sem("norm_ready")
        high_ready = sem("high_ready")
        low_ready = sem("low_ready")
        high2_ready = sem("high2_ready")
        operands_ready = sem("operands_ready")
        inside_ready = sem("inside_ready")
        conv_done = sem("conv_done")
        qkv_ready = sem("qkv_ready")
        gate_done = sem("gate_done")
        v_t_done = sem("v_t_done")
        scores_done = sem("scores_done")
        max_ready = sem("max_ready")
        masked = sem("masked")
        shifted = sem("shifted")
        exp_ready = sem("exp_ready")
        total_ready = sem("total_ready")
        inv_ready = sem("inv_ready")
        probs_ready = sem("probs_ready")
        probs_t_ready = sem("probs_t_ready")
        v_t_ready = sem("v_t_ready")
        gate_biased = sem("gate_biased")
        gate_ready = sem("gate_ready")
        table_loaded = sem("table_loaded")
        mix_done = sem("mix_done")
        mixed_ready = sem("mixed_ready")
        proj_done = sem("proj_done")
        out_ready = sem("out_ready")
        stored = sem("stored")

        def patch(s, r0, c0, rows, cols):
            row = ((s >> BAND_SHIFT) & (PAIRS * BANDS - 1)) * BAND
            row = row + ((s >> PAIR_SHIFT) & (PAIRS - 1)) * 2
            return Xr[:, bass.ds(row + r0, rows), bass.ds((s & (STRIPS - 1)) * STRIP + c0, cols)]

        block = ctx.enter_context(nc.Block())

        @block.sync
        def _(sp):
            sp.dma_start(w_dw_b, w_dw_rows).then_inc(w_dw_in, 16)
            sp.dma_start(b_both, biases).then_inc(weights_in, 16)
            sp.dma_start(spare[bias, 2 * QKV:4 * QKV], bias_rows).then_inc(weights_in, 16)
            halves = x.rearrange("(j b) c h w -> j (b c) h w", j=PAIRS)
            at = 0
            for n, rows in enumerate(CHUNK_ROWS):
                sp.dma_start(Xv[:, 0, 1 + at:1 + at + rows, 1:1 + W],
                             halves[0, :, at:at + rows, :]).then_inc(x_in[n], 16)
                at += rows
            rows = H // CHUNKS
            for n in range(CHUNKS):
                sp.dma_start(Xv[:, 1, 1 + n * rows:1 + (n + 1) * rows, 1:1 + W],
                             halves[1, :, n * rows:(n + 1) * rows, :]).then_inc(x_in_next, 16)
            bands = out.rearrange("(j b) c h w -> j (b c) h w", j=PAIRS)

            def store(j, i, k):
                sp.wait_ge(out_ready, (i * 2 + (j * BANDS + k + 1)) * STRIPS)
                sp.wait_ge(stored, (i * 2 + (j * BANDS + k + 2)) * 16)
                sp.dma_start(bands[j, :, bass.ds((i * 2 + k) * BAND, BAND), :], staged[:, k]).then_inc(stored, 16)

            for j in range(PAIRS):
                with sp.Fori(0, BANDS // 2 - j) as i:
                    for k in range(2):
                        store(j, i, k)
            store(PAIRS - 1, BANDS // 2 - 1, 0)
            parts = (slice(0, STRIPS - 2), slice(STRIPS - 2, STRIPS - 1), slice(STRIPS - 1, STRIPS))
            for strips in parts:
                sp.wait_ge(out_ready, STEPS - STRIPS + strips.stop)
                columns = slice(strips.start * STRIP, strips.stop * STRIP)
                sp.dma_start(bands[PAIRS - 1, :, H - BAND:H, columns], staged[:, 1, :, columns]).then_inc(stored, 16)
            sp.wait_ge(stored, 16 * (2 + PAIRS * BANDS - 1 + len(parts)))

        @block.gpsimd
        def _(pool):
            def bias_weights():
                def link(n, ins):
                    ins.then_inc(bias_chain, 1)
                    pool.wait_ge(bias_chain, n)

                pool.wait_ge(consts_in, 16 * 2)
                a = bias_a[bias]
                link(1, nc.gpsimd.tensor_tensor(a, a, bias_d[bias], ALU.mult))
                link(2, nc.gpsimd.tensor_tensor(a, a, temper[bias], ALU.mult))
                link(3, nc.gpsimd.tensor_tensor(a, a, inv_chan[bias], ALU.mult))
                link(4, nc.gpsimd.tensor_copy(bias_hi, a))
                link(5, nc.gpsimd.tensor_tensor(bias_lo, a, bias_hi, ALU.subtract))
                over = [BIAS_ROWS, QKV]
                link(6, nc.gpsimd.tensor_tensor(bias_hi_f, bias_hi, split[bias, 0:1].to_broadcast(over), ALU.mult))
                link(7, nc.gpsimd.tensor_tensor(bias_lo, bias_lo, split[bias, 1:2].to_broadcast(over), ALU.mult))
                nc.gpsimd.tensor_tensor(conv_w[bias, 13, :], bias_lo, bias_hi_f, ALU.add).then_inc(biases_used, 1)
                pool.wait_ge(biases_used, 1)

            nc.gpsimd.memset(Xv[:, :, 0:H + 2:H + 1, :], 0.0)
            nc.gpsimd.memset(Xv[:, :, 1:H + 1, 0:PW:PW - 1], 0.0).then_inc(borders_clear, 1)
            nc.gpsimd.memset(small[:, 6:7], 0.0).then_inc(stored, 32)
            pool.wait_ge(w_dw_in, 16)
            pool.wait_ge(weights_in, 16 * 3)
            nc.gpsimd.tensor_tensor(w_t, w_t, temper, ALU.mult).then_inc(w_tempered, 1)
            pool.wait_ge(w_tempered, 1)
            nc.gpsimd.partition_all_reduce(w_max, w_t, P, ABSMAX).then_inc(w_max_ready, 1)
            over = [P, TAPS, QKV]
            wf = w_full.rearrange(by_tap, t=TAPS)
            nc.gpsimd.tensor_tensor(wf, w_dw_b.rearrange(by_tap, t=TAPS), w_t.unsqueeze(1).to_broadcast(over),
                                    ALU.mult).then_inc(w_product, 1)
            pool.wait_ge(w_product, 1)
            pool.wait_ge(chan_ready, 1)
            nc.gpsimd.tensor_tensor(wf, wf, inv_chan.unsqueeze(1).to_broadcast(over), ALU.mult).then_inc(w_scaled, 1)
            pool.wait_ge(w_scaled, 1)
            bias_weights()
            pool.wait_ge(w_high_ready, 1)
            nc.gpsimd.tensor_tensor(low_w, w_full, high_w, ALU.subtract).then_inc(low_w_ready, 1)
            pool.wait_ge(low_w_ready, 1)

            def inside(s, k):
                wait(pool, conv_done, (s - 1) * GROUPS)
                r = in_rows[bias, bass.ds(((s >> BAND_SHIFT) & (BANDS - 1)) * BAND, BAND)]
                c = in_cols[bias, bass.ds((s & (STRIPS - 1)) * STRIP, STRIP)].rearrange("p (g c) -> p g c", c=GW)
                over = [BIAS_ROWS, GROUPS, BAND, GW]
                for t in range(2):
                    last = nc.gpsimd.tensor_tensor(
                        low2inside[bias, k, t].rearrange("p g (r c) -> p g r c", c=GW),
                        r.unsqueeze(1).unsqueeze(3).to_broadcast(over), c.unsqueeze(2).to_broadcast(over), ALU.mult)
                last.then_inc(inside_ready, 1)

            inside(0, 0)
            inside(1, 1)
            with pool.Fori(1, STEPS // 2) as i:
                for k in range(2):
                    inside(i * 2 + k, k)

        @block.scalar
        def _(act):
            act.dma_start(scratch[:, 2 * TAPS * QKV:2 * TAPS * QKV + SCALED], w_qkv_scale).then_inc(weights_in, 16)
            act.dma_start(consts[:], weights).then_inc(consts_in, 16)
            act.dma_start(inside_rc[bias], inside_c).then_inc(consts_in, 16)

            def conv_weights():
                act.wait_ge(w_scaled, 1)
                act.wait_ge(chan_ready, 1)
                nc.scalar.activation(high_w, w_full, ACT.Copy).then_inc(w_high_ready, 1)
                act.wait_ge(w_high_ready, 1)
                hw, lw = (w.rearrange("p (y x o) -> p y x o", y=3, x=3) for w in (high_w, low_w))
                up, down = slice(0, C), slice(C, P)
                for first, half, of, col in ((0, up, hw, 0), (0, down, hw, 1), (6, up, hw, 2), (6, down, hw, 0),
                                             (9, down, hw, 1), (3, up, lw, 0), (3, down, lw, 1), (9, up, lw, 2)):
                    if of is lw:
                        act.wait_ge(low_w_ready, 1)
                    nc.scalar.activation(conv_w[half, first:first + 3, :], of[half, :, col, :], ACT.Copy)
                nc.scalar.activation(conv_w[up, 12, :], hw[up, 0, 2, :], ACT.Copy)
                nc.scalar.activation(conv_w[down, 12, :], hw[down, 1, 2, :], ACT.Copy)
                nc.scalar.activation(conv_w[up, 13, :], hw[up, 2, 2, :], ACT.Copy).then_inc(conv_w_ready, 1)

            def deviation(n):
                act.wait_ge(var_ready, n)
                nc.scalar.activation(small[:, 3:4], small[:, 2:3], ACT.Sqrt).then_inc(dev_ready, 1)

            def high(s):
                act.wait_ge(norm_ready, s + 1)
                wait(act, operands_ready, s * 2)
                wait(act, high2_ready, s * 2)
                nc.scalar.activation(high_n[:], T[:], ACT.Copy).then_inc(high_ready, 1)

            def high2(s, k):
                act.wait_ge(high_ready, s + 1)
                wait(act, conv_done, (s - 1) * GROUPS)
                for t in range(2):
                    of = high_n[t * C:(t + 1) * C, :, 2:2 + STRIP].rearrange("p r (g c) -> p g r c", c=GW)
                    for to in (high2low0, high2low1):
                        last = nc.scalar.activation(to[0:C, k, t].rearrange("p g (r c) -> p g r c", c=GW), of,
                                                    ACT.Copy)
                    last.then_inc(high2_ready, 1)

            def evacuate(s, k, g):
                act.wait_ge(conv_done, s * GROUPS + (g + 1))
                wait(act, v_t_done, s - 1)
                nc.scalar.activation(qkv[:, k, g].rearrange("p k t c -> p t k c"),
                                     conv_ps[g % 2][:, 0:2 * QKV].rearrange("p (t k c) -> p t k c", t=2, k=3),
                                     ACT.Copy).then_inc(qkv_ready, 1)

            def v_up(s):
                act.wait_ge(v_t_done, s)
                wait(act, mix_done, s - 1)
                nc.scalar.activation(v_t[:], v_t_ps[:], ACT.Identity, scale=v_scale[:, 0:1]).then_inc(v_t_ready, 1)

            def exponent(s):
                act.wait_ge(shifted, s)
                nc.scalar.activation(scores[:], scores[:], ACT.Exp, scale=score_scale[:, 0:1]).then_inc(exp_ready, 1)

            def gelu(s):
                act.wait_ge(gate_biased, s)
                nc.scalar.activation(gate[:], gate[:], ACT.Gelu).then_inc(gate_ready, 1)
                wait(act, table_loaded, s - 1)
                nc.scalar.activation(small[:, 7:8], small[:, 6:7], ACT.Exp).then_inc(table_loaded, 1)

            def step(s, k, conv=True, follow=True, prepare=True, attend=True, new_pair=0):
                if conv:
                    evacuate(s, k, 0)
                if follow:
                    high2(s + 1, 1 - k)
                if attend:
                    exponent(s)
                if conv:
                    evacuate(s, k, 1)
                if attend:
                    v_up(s)
                if conv:
                    evacuate(s, k, 2)
                    evacuate(s, k, 3)
                if new_pair:
                    deviation(new_pair)
                if prepare:
                    high(s + 2)
                if attend:
                    gelu(s)

            conv_weights()
            deviation(1)
            high(0)
            high2(0, 0)
            high(1)
            step(0, 0, attend=False)
            act.wait_ge(setup, SCALES_SET)
            step(1, 1)
            with act.Fori(1, (PAIR_STEPS - 2) // 2) as i:
                for k in range(2):
                    step(i * 2 + k, k)
            step(PAIR_STEPS - 2, 0, new_pair=2)
            step(PAIR_STEPS - 1, 1)
            with act.Fori(PAIR_STEPS // 2, STEPS // 2 - 1) as i:
                for k in range(2):
                    step(i * 2 + k, k)
            step(STEPS - 2, 0, prepare=False)
            step(STEPS - 1, 1, follow=False, prepare=False)
            step(STEPS, 0, conv=False, follow=False, prepare=False)

        @block.vector
        def _(dve):
            count = [0]

            def link(ins):
                count[0] += 1
                ins.then_inc(setup, 1)
                dve.wait_ge(setup, count[0])

            def statistics(pair, n):
                rows = Xr[:, bass.ds(n * STAT_ROWS + (pair * (H + 2) + 1), STAT_ROWS), 1:1 + W]
                return nc.vector.bn_stats(stats[:, bass.ds(n, 1), :], rows)

            def means(pair):
                if pair:
                    dve.wait_ge(norm_ready, PAIR_STEPS)
                link(nc.vector.bn_aggr(mean_var[:], stats[:].rearrange("p n k -> p (n k)")))

            def centre(pair):
                dve.wait_ge(group_mean_done, pair + 1)
                nc.vector.tensor_copy(norm[:, 0:1], proj_ps[:, 0:1]).then_inc(norm_chain, 1)
                dve.wait_ge(norm_chain, pair * NORM_LINKS + 1)
                nc.vector.tensor_tensor(small[:, 0:1], mean_var[:, 0:1], norm[:, 0:1],
                                        ALU.subtract).then_inc(norm_chain, 1)
                dve.wait_ge(norm_chain, pair * NORM_LINKS + 2)
                nc.vector.scalar_tensor_tensor(small[:, 1:2], small[:, 0:1], small[:, 0:1], mean_var[:, 1:2],
                                               op0=ALU.mult, op1=ALU.add).then_inc(centred, 1)

            def variance(pair):
                dve.wait_ge(group_var_done, pair + 1)
                nc.vector.tensor_scalar(small[:, 2:3], proj_ps[:, 1:2], EPS, None, ALU.add).then_inc(var_ready, 1)

            def normaliser(pair):
                dve.wait_ge(dev_ready, pair + 1)
                nc.vector.reciprocal(small[:, 4:5], small[:, 3:4]).then_inc(norm_chain, 1)
                dve.wait_ge(norm_chain, pair * NORM_LINKS + 3)
                nc.vector.scalar_tensor_tensor(small[:, 5:6], small[:, 4:5], small[:, 4:5], small[:, 2:3],
                                               op0=ALU.mult, op1=ALU.mult).then_inc(norm_chain, 1)
                dve.wait_ge(norm_chain, pair * NORM_LINKS + 4)
                nc.vector.tensor_scalar(small[:, 5:6], small[:, 5:6], -0.5 * XSCALE, 1.5 * XSCALE,
                                        ALU.mult, ALU.add).then_inc(norm_chain, 1)
                dve.wait_ge(norm_chain, pair * NORM_LINKS + 5)
                nc.vector.tensor_tensor(norm[:, 1:2], small[:, 4:5], small[:, 5:6], ALU.mult).then_inc(norm_chain, 1)
                dve.wait_ge(borders_clear, 1)
                for edge in (Xv[:, pair, 0:H + 2:H + 1, :], Xv[:, pair, 1:H + 1, 0:PW:PW - 1]):
                    last = nc.vector.tensor_scalar(edge, edge, norm[:, 0:1], None, ALU.add)
                last.then_inc(norm_chain, 1)
                dve.wait_ge(norm_chain, (pair + 1) * NORM_LINKS)

            def normalise(s):
                wait(dve, high_ready, s)
                wait(dve, operands_ready, s * 2)
                nc.vector.tensor_scalar(T[:], patch(s, 0, 0, HR, HC), norm[:, 0:1], norm[:, 1:2],
                                        ALU.subtract, ALU.mult).then_inc(norm_ready, 1)

            def low(s):
                dve.wait_ge(high_ready, s + 1)
                nc.vector.tensor_tensor(low_n[:], T[:], high_n[:], ALU.subtract).then_inc(low_ready, 1)

            def operands(s, k, t):
                dve.wait_ge(low_ready, s + 1)
                wait(dve, conv_done, (s - 1) * GROUPS)
                upper, lower = slice(0, C), slice(C, P)
                image = slice(t * C, t * C + C)
                for to, half, of, col, row in (
                        (high01, upper, high_n, 0, 0), (high01, lower, high_n, 1, 0),
                        (high2low0, lower, low_n, 0, 0), (high2low1, lower, low_n, 1, 0),
                        (low2rows, upper, low_n, 2, 0), (low2rows, lower, low_n, 2, 1),
                        (low2inside, upper, low_n, 2, 2)):
                    to = to[half, k, t].rearrange("p g (r c) -> p g r c", c=GW)
                    of = of[image, row:row + to.shape[2], col:col + STRIP]
                    last = nc.vector.tensor_copy(to, of.rearrange("p r (g c) -> p g r c", c=GW))
                last.then_inc(operands_ready, 1)

            def mix(s):
                dve.wait_ge(mix_done, s - 1)
                dve.wait_ge(gate_ready, s - 1)
                wait(dve, proj_done, s - 2)
                nc.vector.tensor_tensor(
                    mixed[:].rearrange("p r (g c) -> p g r c", g=GROUPS),
                    mix_ps[:].rearrange("p (g r c) -> p g r c", g=GROUPS, c=GW),
                    gate[:].rearrange("p (g r c) -> p g r c", g=GROUPS, c=GW), ALU.mult).then_inc(mixed_ready, 1)

            def scores_up(s):
                dve.wait_ge(scores_done, s)
                wait(dve, probs_t_ready, s - 1)
                over = [P, WINDOWS, C]
                nc.vector.tensor_tensor(scores[:], scores_ps[:].rearrange("p (w c) -> p w c", c=C),
                                        other_head.unsqueeze(1).to_broadcast(over), ALU.add).then_inc(masked, 1)
                dve.wait_ge(masked, s)
                nc.vector.tensor_reduce(neg_max[:], scores[:], AX_X, ALU.max, negate=True).then_inc(max_ready, 1)
                dve.wait_ge(max_ready, s)
                nc.vector.tensor_tensor(scores[:], scores[:], neg_max[:].unsqueeze(2).to_broadcast(over),
                                        ALU.add).then_inc(shifted, 1)

            def gate_up(s):
                dve.wait_ge(gate_done, s)
                wait(dve, mixed_ready, s - 1)
                nc.vector.scalar_tensor_tensor(
                    gate[:].rearrange("p (w y) -> p w y", y=HW), gate_ps[:].rearrange("p (w y) -> p w y", y=HW),
                    v_scale[:, 0:1], b_mlp.unsqueeze(1).to_broadcast([P, WINDOWS, HW]), op0=ALU.mult,
                    op1=ALU.add).then_inc(gate_biased, 1)

            def divide(s):
                dve.wait_ge(exp_ready, s)
                nc.vector.tensor_reduce(total[:], scores[:], AX_X, ALU.add).then_inc(total_ready, 1)
                dve.wait_ge(total_ready, s)
                nc.vector.reciprocal(inv_total[:], total[:]).then_inc(inv_ready, 1)
                dve.wait_ge(inv_ready, s)
                nc.vector.tensor_tensor(scores[:], scores[:],
                                        inv_total[:].unsqueeze(2).to_broadcast([P, WINDOWS, C]),
                                        ALU.mult).then_inc(probs_ready, 1)

            def turn(s):
                dve.wait_ge(probs_ready, s)
                wait(dve, mix_done, s - 1)
                for u in range(2):
                    for t in range(2):
                        last = nc.vector.transpose(
                            probs_t[t * C:(t + 1) * C, :, u, :],
                            scores[u * C:(u + 1) * C].rearrange("p (g t) d -> p g t d", t=2)[:, :, t, :])
                last.then_inc(probs_t_ready, 1)

            def residual(s):
                r = s - 2
                dve.wait_ge(proj_done, s - 1)
                dve.wait_ge(stored, ((r >> BAND_SHIFT) + 1) * 16)
                to = staged[:].rearrange("p a r w -> p (a r) w")
                to = to[:, bass.ds(((r >> BAND_SHIFT) & 1) * BAND, BAND), bass.ds((r & (STRIPS - 1)) * STRIP, STRIP)]
                nc.vector.scalar_tensor_tensor(to, proj_ps[:].rearrange("p (r c) -> p r c", c=STRIP), b_proj,
                                               patch(r, 1, 1, BAND, STRIP), op0=ALU.add,
                                               op1=ALU.add).then_inc(out_ready, 1)

            def step(s, k, prepare=True, attend=True, finish=True, ahead=True, more=(), new_pair=0):
                if new_pair:
                    means(new_pair)
                if prepare:
                    low(s + 1)
                    operands(s + 1, 1 - k, 0)
                if finish:
                    mix(s)
                if attend:
                    scores_up(s)
                    gate_up(s)
                    divide(s)
                    turn(s)
                if new_pair:
                    centre(new_pair)
                if prepare:
                    operands(s + 1, 1 - k, 1)
                if new_pair:
                    variance(new_pair)
                    normaliser(new_pair)
                for pair, n in more:
                    statistics(pair, n)
                if ahead:
                    normalise(s + 2)
                if finish:
                    residual(s)

            def scales():
                dve.wait_ge(w_dw_in, 16)
                link(nc.vector.tensor_reduce(dw_max, w_dw_b.rearrange("p (t o) -> p o t", t=TAPS), AX_X, ALU.max,
                                             apply_absolute_value=True))
                dve.wait_ge(weights_in, 16 * 3)
                over = b_both.rearrange("p (n o) -> p n o", n=2)
                link(nc.vector.tensor_tensor(over, over, temper.unsqueeze(1).to_broadcast([P, 2, QKV]), ALU.mult))
                link(nc.vector.scalar_tensor_tensor(b_both, b_both, -1.0, b_both, op0=ALU.mult, op1=ALU.max))
                dve.wait_ge(w_max_ready, 1)
                link(nc.vector.tensor_tensor(chan, w_max, b_qkv_b, ALU.max))
                link(nc.vector.tensor_tensor(chan, chan, dw_max, ALU.mult))
                link(nc.vector.tensor_tensor(chan, chan, b_dw_b, ALU.max))
                link(nc.vector.tensor_scalar(chan, chan, TINY, 1.0 / WSCALE, ALU.max, ALU.mult))
                link(nc.vector.tensor_reduce(small[:, 5:6], chan[:, C:2 * C], AX_X, ALU.max))
                link(nc.vector.tensor_scalar(chan[:, C:2 * C], chan[:, C:2 * C], 0.0, small[:, 5:6],
                                             ALU.mult, ALU.add))
                nc.vector.reciprocal(inv_chan, chan).then_inc(chan_ready, 1)

            def scale_columns():
                for part, column in ((0, score_scale), (2, v_scale)):
                    for half in (slice(0, C), slice(C, P)):
                        last = nc.vector.tensor_tensor(diagonal[half], chan[half, part * C:(part + 1) * C],
                                                       ident[half, half], ALU.mult)
                    link(last)
                    link(nc.vector.tensor_reduce(column[:], diagonal, AX_X, ALU.add))
                unscale = 1.0 / XSCALE
                link(nc.vector.tensor_scalar(v_scale[:], v_scale[:], unscale, None, ALU.mult))
                link(nc.vector.tensor_scalar(score_scale[:], score_scale[:], unscale * unscale, chan[:, C:C + 1],
                                             ALU.mult, ALU.mult))

            scales()
            piece = 0
            for n, rows in enumerate(CHUNK_ROWS):
                dve.wait_ge(x_in[n], 16)
                for _ in range(rows // STAT_ROWS):
                    last = statistics(0, piece)
                    piece += 1
            link(last)
            means(0)
            assert count[0] == MEANS_SET, count
            centre(0)
            variance(0)
            normaliser(0)
            normalise(0)
            low(0)
            operands(0, 0, 0)
            operands(0, 0, 1)
            normalise(1)
            scale_columns()
            assert count[0] == SCALES_SET, count
            step(0, 0, attend=False, finish=False)
            step(1, 1, finish=False)
            singles = 2 * (PAIR_STEPS - 4) - STATS
            dve.wait_ge(x_in_next, 16 * CHUNKS)
            with dve.Fori(1, 1 + singles // 2) as i:
                for k in range(2):
                    step(i * 2 + k, k, more=[(1, i * 2 + (k - 2))])
            with dve.Fori(1 + singles // 2, (PAIR_STEPS - 2) // 2) as i:
                for k in range(2):
                    step(i * 2 + k, k, more=[(1, i * 4 + (2 * k + m - singles - 4)) for m in range(2)])
            step(PAIR_STEPS - 2, 0, new_pair=1)
            step(PAIR_STEPS - 1, 1)
            with dve.Fori(PAIR_STEPS // 2, STEPS // 2 - 1) as i:
                for k in range(2):
                    step(i * 2 + k, k)
            step(STEPS - 2, 0, ahead=False)
            step(STEPS - 1, 1, prepare=False, ahead=False)
            step(STEPS, 0, prepare=False, ahead=False)
            step(STEPS + 1, 1, prepare=False, attend=False, ahead=False)

        @block.tensor
        def _(pe):
            def group_mean_of(pair):
                pe.wait_ge(setup, MEANS_SET if pair == 0 else SCALES_SET + 1)
                wait(pe, out_ready, 0 if pair == 0 else PAIR_STEPS - 4)
                nc.tensor.matmul(proj_ps[:, 0:1], group_mean, mean_var[:, 0:1], start=True,
                                 stop=True).then_inc(group_mean_done, 1)

            def group_var_of(pair):
                pe.wait_ge(centred, pair + 1)
                nc.tensor.matmul(proj_ps[:, 1:2], group_mean, small[:, 1:2], start=True,
                                 stop=True).then_inc(group_var_done, 1)

            def keep_clock_up(products):
                for _ in range(products):
                    nc.tensor.matmul(mix_ps[:, 0:QKV], conv_w[:, 0, 0:P], conv_w[:, 0, :], start=True, stop=True)

            def conv(s, k, g):
                if g == 0:
                    pe.wait_ge(inside_ready, s + 1)
                wait(pe, qkv_ready, s * GROUPS + (g - 1))
                for t in range(2):
                    if g == 0:
                        pe.wait_ge(operands_ready, s * 2 + (t + 1))
                        pe.wait_ge(high2_ready, s * 2 + (t + 1))

                    def rows(tensor, y=0, p=P):
                        return tensor[0:p, k, t, g, y * GW:y * GW + NP]
                    passes = [rows(high01, y) for y in range(3)] * 2
                    passes += [rows(high2low0, y) for y in range(3)] + [rows(high2low1, y) for y in range(3)]
                    passes += [rows(low2rows), rows(low2inside, p=C + BIAS_ROWS)]
                    for n, pixels in enumerate(passes):
                        last = nc.tensor.matmul(conv_ps[g % 2][:, t * QKV:(t + 1) * QKV], pixels,
                                                conv_w[0:pixels.shape[0], n, :],
                                                start=(n == 0), stop=(n == len(passes) - 1))
                last.then_inc(conv_done, 1)

            def attend(s, k):
                pe.wait_ge(qkv_ready, s * GROUPS)
                wait(pe, masked, s - 1)
                wait(pe, gate_biased, s - 1)
                for g in range(GROUPS):
                    v = qkv[:, k, g, 2].rearrange("p t c -> p (t c)")
                    last = nc.tensor.matmul(gate_ps[:, g * P:(g + 1) * P], v, mlp, start=True, stop=True)
                last.then_inc(gate_done, 1)
                for g in range(GROUPS):
                    for t in range(2):
                        for u in range(2):
                            h = slice(u * HW, (u + 1) * HW)
                            last = nc.tensor.matmul(
                                scores_ps[u * C:(u + 1) * C, (2 * g + t) * C:(2 * g + t + 1) * C],
                                qkv[h, k, g, 0, t, :], qkv[h, k, g, 1, t, :], start=True, stop=True)
                last.then_inc(scores_done, 1)
                wait(pe, v_t_ready, s - 1)
                for g in range(GROUPS):
                    v = qkv[:, k, g, 2].rearrange("p t c -> p (t c)")
                    last = nc.tensor.transpose(v_t_ps[:, g * P:(g + 1) * P], v, ident)
                last.then_inc(v_t_done, 1)

            def wait_for_probs(s):
                pe.wait_ge(probs_t_ready, s)
                pe.wait_ge(v_t_ready, s)
                wait(pe, mixed_ready, s - 1)

            def apply_probs(s):
                for g in range(GROUPS):
                    for u in range(2):
                        at = slice(g * P + u * HW, g * P + (u + 1) * HW)
                        for t in range(2):
                            h = slice(t * C, (t + 1) * C)
                            last = nc.tensor.matmul(mix_ps[h, at], probs_t[h, g, u, :], v_t[h, at],
                                                    start=True, stop=True)
                last.then_inc(mix_done, 1)

            def project(s):
                pe.wait_ge(mixed_ready, s - 1)
                wait(pe, out_ready, s - 2)
                nc.tensor.matmul(proj_ps[:], proj, mixed[:].rearrange("p r c -> p (r c)"), start=True,
                                 stop=True).then_inc(proj_done, 1)

            def step(s, k, convolve=True, attention=True, finish=True, new_pair=0):
                if convolve:
                    conv(s, k, 0)
                if attention:
                    attend(s, 1 - k)
                if convolve:
                    conv(s, k, 1)
                    conv(s, k, 2)
                if new_pair:
                    group_mean_of(new_pair)
                if attention and not convolve:
                    pe.wait_ge(mixed_ready, s - 1)
                    keep_clock_up(WARM_END)
                if convolve:
                    conv(s, k, 3)
                if new_pair:
                    group_var_of(new_pair)
                    pe.wait_ge(var_ready, new_pair + 1)
                if attention:
                    wait_for_probs(s)
                if finish:
                    project(s)
                if attention:
                    apply_probs(s)

            pe.wait_ge(consts_in, 16 * 2)
            group_mean_of(0)
            group_var_of(0)
            pe.wait_ge(conv_w_ready, 1)
            pe.wait_ge(biases_used, 1)
            keep_clock_up(WARM_START)
            step(0, 0, attention=False, finish=False)
            step(1, 1, finish=False)
            with pe.Fori(1, (PAIR_STEPS - 2) // 2) as i:
                for k in range(2):
                    step(i * 2 + k, k)
            step(PAIR_STEPS - 2, 0, new_pair=1)
            step(PAIR_STEPS - 1, 1)
            with pe.Fori(PAIR_STEPS // 2, STEPS // 2) as i:
                for k in range(2):
                    step(i * 2 + k, k)
            step(STEPS, 0, convolve=False)
            step(STEPS + 1, 1, convolve=False, attention=False)


_ORDER = ("x", "w_dw_rows", "w_qkv_scale", "biases", "bias_rows", "weights", "inside")


def _inside():
    tap = np.arange(16)
    dy, dx = tap // 3 - 1, tap % 3 - 1
    dy[TAPS:], dx[TAPS:] = 0, 0
    at = np.arange(H)
    rows = ((at + dy[:, None] >= 0) & (at + dy[:, None] < H)) * XSCALE
    cols = ((at + dx[:, None] >= 0) & (at + dx[:, None] < W)) * 1.0
    rows[TAPS + 1:] = 0
    return np.tile(np.concatenate([rows, cols], 1), (BIAS_ROWS // 16, 1)).astype(np.float16)


def _other_head():
    head = np.arange(P) % C // (C // HEADS)
    return np.where(head[:, None] == head[None, :C], 0.0, NEG).astype(np.float32)


def kernel(x, L0_conv_w_qkv, L0_conv_b_qkv, L0_conv_w_dw, L0_conv_b_dw, L0_conv_temperature, L0_conv_w_mlp,
           L0_conv_b_mlp, L0_conv_w_proj, L0_conv_b_proj):
    import concourse.bacc as _bacc
    from concourse.bass_utils import run_bass_kernel_spmd as _run

    def two(a):
        z = np.zeros_like(a)
        return np.concatenate([np.concatenate([a, z], 1), np.concatenate([z, a], 1)], 0)

    def everywhere(row):
        return np.broadcast_to(row, (P, row.size))

    w_qkv, w_dw = np.asarray(L0_conv_w_qkv), np.asarray(L0_conv_w_dw).reshape(QKV, TAPS)
    b_qkv, b_dw = np.asarray(L0_conv_b_qkv), np.asarray(L0_conv_b_dw)
    f = w_qkv.dtype
    one, none = np.ones(QKV, f), np.zeros((16 - TAPS - 1, QKV), f)
    bias_a = np.concatenate([np.broadcast_to(b_qkv, (TAPS, QKV)), b_dw[None], none] * (BIAS_ROWS // 16))
    bias_d = np.concatenate([w_dw.T, one[None], none] * (BIAS_ROWS // 16))
    per_head = np.repeat(np.asarray(L0_conv_temperature).reshape(HEADS), C // HEADS)
    temper = np.concatenate([per_head, one[:2 * C]])
    chan = np.arange(P)
    group = (0.5 * (chan[:, None] // 2 == chan[None, :] // 2)).astype(f)
    arrays = {
        "x": np.asarray(x),
        "w_dw_rows": everywhere(np.ascontiguousarray(w_dw.T).reshape(-1)),
        "w_qkv_scale": np.concatenate([np.concatenate([w_qkv.T] * 2), everywhere(temper)], 1),
        "biases": np.concatenate([everywhere(b_qkv), everywhere(b_dw)], 1),
        "bias_rows": np.concatenate([bias_a, bias_d], 1),
        "weights": np.concatenate([
            np.eye(P, dtype=f), group, two(np.asarray(L0_conv_w_mlp).T), two(np.asarray(L0_conv_w_proj).T),
            everywhere(np.asarray(L0_conv_b_mlp)), _other_head(),
            np.concatenate([np.asarray(L0_conv_b_proj)] * 2).reshape(P, 1),
            np.tile(np.repeat(np.eye(2, dtype=f), 16, axis=0), (P // 32, 1))], 1),
        "inside": _inside(),
    }
    nc = _bacc.Bacc("TRN2", target_bir_lowering=False, num_devices=1)
    given, args = {}, []
    for name in _ORDER:
        a = np.ascontiguousarray(arrays[name])
        given[f"in_{name}"] = a
        args.append(nc.dram_tensor(f"in_{name}", a.shape, mybir.dt.from_np(a.dtype), kind="ExternalInput").ap())
    args.append(nc.dram_tensor("out_y", (B, C, H, W), F32, kind="ExternalOutput").ap())
    build(nc, *args)
    return _run(nc, [given], core_ids=[0]).results[0]["out_y"]
```
